# Optimizing a Trainium2 kernel written in Bass

```python
import numpy as np
import jax
import jax.numpy as jnp

def _softmax(x, axis=-1):
    return jax.nn.softmax(x, axis=axis)

def _gelu(x):
    return jax.nn.gelu(x, approximate=True)

def _silu(x):
    return jax.nn.silu(x)

def _sigmoid(x):
    return jax.nn.sigmoid(x)

def _layernorm(x, axis=-1, eps=1e-05):
    m = jnp.mean(x, axis=axis, keepdims=True)
    v = jnp.var(x, axis=axis, keepdims=True)
    return (x - m) / jnp.sqrt(v + eps)

def _scatter_add(tgt, idx, src, axis=0):
    return tgt.at[idx].add(src)

def _segment_sum(src, seg, n):
    return jax.ops.segment_sum(src, seg, n)
kernel_name = 'mk_gnn_resnorm_d4_gnn_r16_b3d7ec'

def setup_inputs(seed: int=0):
    np.random.seed(seed)
    _w = jnp.asarray

    def _rec_inputs():
        import jax
        import jax.numpy as jnp
        _gk = jax.random.key(seed)
        x = -0.0009044 + 1 * jax.random.normal(jax.random.fold_in(_gk, 1), (6250, 16), jnp.float32)
        _s = jax.random.randint(jax.random.fold_in(_gk, 2), (100000,), 0, 6250, jnp.int32)
        _d = jax.random.randint(jax.random.fold_in(_gk, 3), (100000,), 0, 6250, jnp.int32)
        _loop = jnp.arange(6250, dtype=jnp.int32)
        src = jnp.concatenate([_s, _d, _loop])
        dst = jnp.concatenate([_d, _s, _loop])
        _o = jnp.argsort(dst, stable=True)
        src = src[_o]
        dst = dst[_o]
        edge_attr_13 = 2.91757e-06 + 0.999892 * jax.random.normal(jax.random.fold_in(_gk, 12), (206250, 13), jnp.float32)
        edge_attr_8 = -5.3897e-05 + 0.999841 * jax.random.normal(jax.random.fold_in(_gk, 13), (206250, 8), jnp.float32)
        edge_weight1 = jax.random.uniform(jax.random.fold_in(_gk, 15), (206250, 1), jnp.float32, 0.0, 1)
        node_vec1 = -0.00472126 + 0.997171 * jax.random.normal(jax.random.fold_in(_gk, 16), (6250, 1), jnp.float32)
        return (x, src, dst, edge_attr_13, edge_attr_8, edge_weight1, node_vec1)
    x, src, dst, edge_attr_13, edge_attr_8, edge_weight1, node_vec1 = _rec_inputs()

    def _L0_gnn_setup():
        import jax, jax.numpy as jnp
        import numpy as np
        N_NODES = 6250
        N_EDGES = 200000
        D_NODE = 16
        D_EDGE = 8
        D_HIDDEN = 16
        key = jax.random.key(seed)
        ks = jax.random.split(key, 8)
        node_features = jax.random.normal(ks[0], (N_NODES, D_NODE), dtype=jnp.float32)
        edge_attr_e3nn = jax.random.normal(ks[1], (N_EDGES, D_EDGE), dtype=jnp.float32)
        node_attr_scalar_raw = jax.random.normal(ks[2], (N_NODES, 1), dtype=jnp.float32)
        W_msg_tp = jax.random.normal(ks[3], (D_NODE, D_EDGE, D_HIDDEN), dtype=jnp.float32)
        W_msg_lin = jax.random.normal(ks[4], (D_HIDDEN, D_HIDDEN), dtype=jnp.float32)
        W_upd_tp = jax.random.normal(ks[5], (D_NODE, D_HIDDEN, D_HIDDEN), dtype=jnp.float32)
        W_upd_lin = jax.random.normal(ks[6], (D_HIDDEN, D_NODE), dtype=jnp.float32)
        edge_index = jax.random.randint(ks[7], (2, N_EDGES), 0, N_NODES, dtype=jnp.int64)
        return {'node_features': node_features, 'edge_attr_e3nn': edge_attr_e3nn, 'node_attr_scalar_raw': node_attr_scalar_raw, 'W_msg_tp': W_msg_tp, 'W_msg_lin': W_msg_lin, 'W_upd_tp': W_upd_tp, 'W_upd_lin': W_upd_lin, 'edge_index': edge_index}
    _L0_gnn_all = _L0_gnn_setup()
    _L0_gnn_in = {k: v for k, v in _L0_gnn_all.items() if k in ('W_msg_tp', 'W_msg_lin', 'W_upd_tp', 'W_upd_lin')}
    del _L0_gnn_all

    def _L1_gnn_setup():
        import jax, jax.numpy as jnp
        import numpy as np
        N = 3125
        E = 25000
        IN_CH = 16
        SLOPE = 0.01

        def leaky(v):
            return jnp.where(v > 0, v, SLOPE * v)

        def gcn_conv(x, src, dst, W, b, n):
            h = x @ W
            deg = jnp.zeros((n,), x.dtype).at[dst].add(1.0) + 1.0
            dinv = jax.lax.rsqrt(deg)
            norm = dinv[src] * dinv[dst]
            agg = jax.ops.segment_sum(h[src] * norm[:, None], dst, num_segments=n)
            agg = agg + h * (dinv * dinv)[:, None]
            return agg + b
        key = jax.random.key(seed)
        ks = jax.random.split(key, 24)

        def w(k, i, o):
            return jax.random.normal(k, (i, o), jnp.float32) / np.sqrt(i)
        inp = {'x': jax.random.normal(ks[0], (N, IN_CH), jnp.float32), 'edge_index': jax.random.randint(ks[1], (2, E), 0, N, jnp.int64), 'enc_W0': w(ks[2], IN_CH, 64), 'enc_b0': jnp.zeros((64,), jnp.float32), 'enc_W1': w(ks[3], 64, 128), 'enc_b1': jnp.zeros((128,), jnp.float32), 'enc_W2': w(ks[4], 128, 64), 'enc_b2': jnp.zeros((64,), jnp.float32), 'lat_W0': w(ks[5], 64, 32), 'lat_b0': jnp.zeros((32,), jnp.float32), 'lat_W1': w(ks[6], 32, 3), 'lat_b1': jnp.zeros((3,), jnp.float32), 'dfc_W0': w(ks[7], 3, 32), 'dfc_b0': jnp.zeros((32,), jnp.float32), 'dfc_W1': w(ks[8], 32, 64), 'dfc_b1': jnp.zeros((64,), jnp.float32), 'dec_W0': w(ks[9], 64, 128), 'dec_b0': jnp.zeros((128,), jnp.float32), 'dec_W1': w(ks[10], 128, 64), 'dec_b1': jnp.zeros((64,), jnp.float32), 'dec_W2': w(ks[11], 64, IN_CH), 'dec_b2': jnp.zeros((IN_CH,), jnp.float32)}
        return inp
    _L1_gnn_all = _L1_gnn_setup()
    _L1_gnn_in = {k: v for k, v in _L1_gnn_all.items() if k in ('enc_W0', 'enc_b0', 'enc_W1', 'enc_b1', 'enc_W2', 'enc_b2', 'lat_W0', 'lat_b0', 'lat_W1', 'lat_b1', 'dfc_W0', 'dfc_b0', 'dfc_W1', 'dfc_b1', 'dec_W0', 'dec_b0', 'dec_W1', 'dec_b1', 'dec_W2', 'dec_b2')}
    del _L1_gnn_all

    def _L2_gnn_setup():
        import jax, jax.numpy as jnp
        import numpy as np
        N_NODES = 12500
        N_RAND_EDGES = 400000
        D = 16
        key = jax.random.key(seed)
        k1, k2, k3, k4, k5, k6 = jax.random.split(key, 6)
        inputs = jax.random.normal(k1, (N_NODES, D), dtype=jnp.float32)
        src_r = jax.random.randint(k2, (N_RAND_EDGES,), 0, N_NODES, dtype=jnp.int32)
        dst_r = jax.random.randint(k3, (N_RAND_EDGES,), 0, N_NODES, dtype=jnp.int32)
        loop = jnp.arange(N_NODES, dtype=jnp.int32)
        src = jnp.concatenate([src_r, loop])
        dst = jnp.concatenate([dst_r, loop])
        E = src.shape[0]
        timestamp = jax.random.uniform(k4, (E, 1), dtype=jnp.float32)
        W = jax.random.normal(k5, (D, D), dtype=jnp.float32) * (1.0 / np.sqrt(D))
        b = jax.random.normal(k6, (D,), dtype=jnp.float32) * 0.01
        return {'inputs': inputs, 'timestamp': timestamp, 'W': W, 'b': b, 'src': src, 'dst': dst}
    _L2_gnn_all = _L2_gnn_setup()
    _L2_gnn_in = {k: v for k, v in _L2_gnn_all.items() if k in ('W', 'b')}
    del _L2_gnn_all

    def _L3_gnn_setup():
        import jax, jax.numpy as jnp
        import numpy as np
        N = 3125
        E = 50000
        NC = 16
        FDIM = 13
        HID = 32
        NREPEATS = 2

        def _gru_cell(x, h, w_ih, w_hh, b_ih, b_hh):
            gi = x @ w_ih.T + b_ih
            gh = h @ w_hh.T + b_hh
            i_r, i_z, i_n = jnp.split(gi, 3, axis=1)
            h_r, h_z, h_n = jnp.split(gh, 3, axis=1)
            r = jax.nn.sigmoid(i_r + h_r)
            z = jax.nn.sigmoid(i_z + h_z)
            n = jnp.tanh(i_n + r * h_n)
            return (1.0 - z) * n + z * h
        key = jax.random.key(seed)
        ks = jax.random.split(key, 10)
        hx = jax.random.normal(ks[0], (N, NC), dtype=jnp.float32)
        edgefeats = jax.random.normal(ks[1], (E, FDIM), dtype=jnp.float32)
        edge_src = jax.random.randint(ks[2], (E,), 0, N, dtype=jnp.int32)
        edge_dst = jax.random.randint(ks[3], (E,), 0, N, dtype=jnp.int32)
        fnet_w1 = jax.random.normal(ks[4], (FDIM, HID), dtype=jnp.float32) * (1.0 / np.sqrt(FDIM))
        fnet_b1 = jnp.zeros((HID,), dtype=jnp.float32)
        fnet_w2 = jax.random.normal(ks[5], (HID, NC * NC), dtype=jnp.float32) * (0.1 / np.sqrt(HID))
        fnet_b2 = jnp.zeros((NC * NC,), dtype=jnp.float32)
        gru_w_ih = jax.random.normal(ks[6], (3 * NC, NC), dtype=jnp.float32) * (1.0 / np.sqrt(NC))
        gru_w_hh = jax.random.normal(ks[7], (3 * NC, NC), dtype=jnp.float32) * (1.0 / np.sqrt(NC))
        gru_b_ih = jnp.zeros((3 * NC,), dtype=jnp.float32)
        gru_b_hh = jnp.zeros((3 * NC,), dtype=jnp.float32)
        return {'hx': hx, 'edgefeats': edgefeats, 'edge_src': edge_src, 'edge_dst': edge_dst, 'fnet_w1': fnet_w1, 'fnet_b1': fnet_b1, 'fnet_w2': fnet_w2, 'fnet_b2': fnet_b2, 'gru_w_ih': gru_w_ih, 'gru_w_hh': gru_w_hh, 'gru_b_ih': gru_b_ih, 'gru_b_hh': gru_b_hh}
    _L3_gnn_all = _L3_gnn_setup()
    _L3_gnn_in = {k: v for k, v in _L3_gnn_all.items() if k in ('fnet_w1', 'fnet_b1', 'fnet_w2', 'fnet_b2', 'gru_w_ih', 'gru_w_hh', 'gru_b_ih', 'gru_b_hh')}
    del _L3_gnn_all
    return {'x': x, 'src': src, 'dst': dst, 'edge_attr_13': edge_attr_13, 'edge_attr_8': edge_attr_8, 'edge_weight1': edge_weight1, 'node_vec1': node_vec1, 'L0_gnn_W_msg_tp': _L0_gnn_in['W_msg_tp'], 'L0_gnn_W_msg_lin': _L0_gnn_in['W_msg_lin'], 'L0_gnn_W_upd_tp': _L0_gnn_in['W_upd_tp'], 'L0_gnn_W_upd_lin': _L0_gnn_in['W_upd_lin'], 'L1_gnn_enc_W0': _L1_gnn_in['enc_W0'], 'L1_gnn_enc_b0': _L1_gnn_in['enc_b0'], 'L1_gnn_enc_W1': _L1_gnn_in['enc_W1'], 'L1_gnn_enc_b1': _L1_gnn_in['enc_b1'], 'L1_gnn_enc_W2': _L1_gnn_in['enc_W2'], 'L1_gnn_enc_b2': _L1_gnn_in['enc_b2'], 'L1_gnn_lat_W0': _L1_gnn_in['lat_W0'], 'L1_gnn_lat_b0': _L1_gnn_in['lat_b0'], 'L1_gnn_lat_W1': _L1_gnn_in['lat_W1'], 'L1_gnn_lat_b1': _L1_gnn_in['lat_b1'], 'L1_gnn_dfc_W0': _L1_gnn_in['dfc_W0'], 'L1_gnn_dfc_b0': _L1_gnn_in['dfc_b0'], 'L1_gnn_dfc_W1': _L1_gnn_in['dfc_W1'], 'L1_gnn_dfc_b1': _L1_gnn_in['dfc_b1'], 'L1_gnn_dec_W0': _L1_gnn_in['dec_W0'], 'L1_gnn_dec_b0': _L1_gnn_in['dec_b0'], 'L1_gnn_dec_W1': _L1_gnn_in['dec_W1'], 'L1_gnn_dec_b1': _L1_gnn_in['dec_b1'], 'L1_gnn_dec_W2': _L1_gnn_in['dec_W2'], 'L1_gnn_dec_b2': _L1_gnn_in['dec_b2'], 'L2_gnn_W': _L2_gnn_in['W'], 'L2_gnn_b': _L2_gnn_in['b'], 'L3_gnn_fnet_w1': _L3_gnn_in['fnet_w1'], 'L3_gnn_fnet_b1': _L3_gnn_in['fnet_b1'], 'L3_gnn_fnet_w2': _L3_gnn_in['fnet_w2'], 'L3_gnn_fnet_b2': _L3_gnn_in['fnet_b2'], 'L3_gnn_gru_w_ih': _L3_gnn_in['gru_w_ih'], 'L3_gnn_gru_w_hh': _L3_gnn_in['gru_w_hh'], 'L3_gnn_gru_b_ih': _L3_gnn_in['gru_b_ih'], 'L3_gnn_gru_b_hh': _L3_gnn_in['gru_b_hh']}

def reference(x, src, dst, edge_attr_13, edge_attr_8, edge_weight1, node_vec1, L0_gnn_W_msg_tp, L0_gnn_W_msg_lin, L0_gnn_W_upd_tp, L0_gnn_W_upd_lin, L1_gnn_enc_W0, L1_gnn_enc_b0, L1_gnn_enc_W1, L1_gnn_enc_b1, L1_gnn_enc_W2, L1_gnn_enc_b2, L1_gnn_lat_W0, L1_gnn_lat_b0, L1_gnn_lat_W1, L1_gnn_lat_b1, L1_gnn_dfc_W0, L1_gnn_dfc_b0, L1_gnn_dfc_W1, L1_gnn_dfc_b1, L1_gnn_dec_W0, L1_gnn_dec_b0, L1_gnn_dec_W1, L1_gnn_dec_b1, L1_gnn_dec_W2, L1_gnn_dec_b2, L2_gnn_W, L2_gnn_b, L3_gnn_fnet_w1, L3_gnn_fnet_b1, L3_gnn_fnet_w2, L3_gnn_fnet_b2, L3_gnn_gru_w_ih, L3_gnn_gru_w_hh, L3_gnn_gru_b_ih, L3_gnn_gru_b_hh):
    import jax
    import jax.numpy as jnp

    def _L0_gnn_ref(node_features, edge_attr_e3nn, node_attr_scalar_raw, W_msg_tp, W_msg_lin, W_upd_tp, W_upd_lin, edge_index):
        import jax, jax.numpy as jnp
        import numpy as np
        N_NODES = 6250
        N_EDGES = 200000
        D_NODE = 16
        D_EDGE = 8
        D_HIDDEN = 16
        n_nodes = node_features.shape[0]
        row = edge_index[0]
        col = edge_index[1]
        norm_msg_tp = 1.0 / np.float32(np.sqrt(D_NODE * D_EDGE))
        norm_upd_tp = 1.0 / np.float32(np.sqrt(D_NODE * D_HIDDEN))
        norm_lin = 1.0 / np.float32(np.sqrt(D_HIDDEN))
        x_j = node_features[col]
        m = jnp.einsum('ei,ej,ijh->eh', x_j, edge_attr_e3nn, W_msg_tp) * norm_msg_tp
        m = jax.nn.silu(m)
        m = m @ W_msg_lin * norm_lin
        agg = jax.ops.segment_sum(m, row, num_segments=n_nodes)
        u = jnp.einsum('ni,nh,ihk->nk', node_features, agg, W_upd_tp) * norm_upd_tp
        u = jax.nn.silu(u)
        u = u @ W_upd_lin * norm_lin
        return node_features + u

    def _L1_gnn_ref(x, edge_index, enc_W0, enc_b0, enc_W1, enc_b1, enc_W2, enc_b2, lat_W0, lat_b0, lat_W1, lat_b1, dfc_W0, dfc_b0, dfc_W1, dfc_b1, dec_W0, dec_b0, dec_W1, dec_b1, dec_W2, dec_b2):
        import jax, jax.numpy as jnp
        import numpy as np
        N = 3125
        E = 25000
        IN_CH = 16
        SLOPE = 0.01

        def leaky(v):
            return jnp.where(v > 0, v, SLOPE * v)

        def gcn_conv(x, src, dst, W, b, n):
            h = x @ W
            deg = jnp.zeros((n,), x.dtype).at[dst].add(1.0) + 1.0
            dinv = jax.lax.rsqrt(deg)
            norm = dinv[src] * dinv[dst]
            agg = jax.ops.segment_sum(h[src] * norm[:, None], dst, num_segments=n)
            agg = agg + h * (dinv * dinv)[:, None]
            return agg + b
        src, dst = (edge_index[0], edge_index[1])
        n = x.shape[0]
        h = leaky(gcn_conv(x, src, dst, enc_W0, enc_b0, n))
        h = leaky(gcn_conv(h, src, dst, enc_W1, enc_b1, n))
        h = leaky(gcn_conv(h, src, dst, enc_W2, enc_b2, n))
        h = leaky(h @ lat_W0 + lat_b0)
        h = h @ lat_W1 + lat_b1
        h = leaky(h @ dfc_W0 + dfc_b0)
        h = leaky(h @ dfc_W1 + dfc_b1)
        h = leaky(gcn_conv(h, src, dst, dec_W0, dec_b0, n))
        h = leaky(gcn_conv(h, src, dst, dec_W1, dec_b1, n))
        h = leaky(gcn_conv(h, src, dst, dec_W2, dec_b2, n))
        return jnp.tanh(h)

    def _L2_gnn_ref(inputs, timestamp, W, b, src, dst):
        import jax, jax.numpy as jnp
        import numpy as np
        N_NODES = 12500
        N_RAND_EDGES = 400000
        D = 16
        msg = inputs[src] * timestamp
        h = jax.ops.segment_max(msg, dst, num_segments=inputs.shape[0])
        return h @ W.T + b

    def _L3_gnn_ref(hx, edgefeats, edge_src, edge_dst, fnet_w1, fnet_b1, fnet_w2, fnet_b2, gru_w_ih, gru_w_hh, gru_b_ih, gru_b_hh):
        import jax, jax.numpy as jnp
        import numpy as np
        N = 3125
        E = 50000
        NC = 16
        FDIM = 13
        HID = 32
        NREPEATS = 2

        def _gru_cell(x, h, w_ih, w_hh, b_ih, b_hh):
            gi = x @ w_ih.T + b_ih
            gh = h @ w_hh.T + b_hh
            i_r, i_z, i_n = jnp.split(gi, 3, axis=1)
            h_r, h_z, h_n = jnp.split(gh, 3, axis=1)
            r = jax.nn.sigmoid(i_r + h_r)
            z = jax.nn.sigmoid(i_z + h_z)
            n = jnp.tanh(i_n + r * h_n)
            return (1.0 - z) * n + z * h
        n_nodes, nc = hx.shape
        w = jax.nn.relu(edgefeats @ fnet_w1 + fnet_b1) @ fnet_w2 + fnet_b2
        W = w.reshape(-1, nc, nc)
        deg = jax.ops.segment_sum(jnp.ones((edge_dst.shape[0],), hx.dtype), edge_dst, num_segments=n_nodes)
        inv_deg = 1.0 / jnp.maximum(deg, 1.0)
        for _ in range(NREPEATS):
            xj = hx[edge_src]
            m = jnp.einsum('ei,eio->eo', xj, W)
            agg = jax.ops.segment_sum(m, edge_dst, num_segments=n_nodes)
            agg = agg * inv_deg[:, None]
            hx = _gru_cell(agg, hx, gru_w_ih, gru_w_hh, gru_b_ih, gru_b_hh)
        return hx
    edge_index = jnp.stack([src, dst])
    x = _layernorm(x + _L0_gnn_ref(x, edge_attr_8, node_vec1, L0_gnn_W_msg_tp, L0_gnn_W_msg_lin, L0_gnn_W_upd_tp, L0_gnn_W_upd_lin, edge_index), axis=-1)
    x = _layernorm(x + _L1_gnn_ref(x, edge_index, L1_gnn_enc_W0, L1_gnn_enc_b0, L1_gnn_enc_W1, L1_gnn_enc_b1, L1_gnn_enc_W2, L1_gnn_enc_b2, L1_gnn_lat_W0, L1_gnn_lat_b0, L1_gnn_lat_W1, L1_gnn_lat_b1, L1_gnn_dfc_W0, L1_gnn_dfc_b0, L1_gnn_dfc_W1, L1_gnn_dfc_b1, L1_gnn_dec_W0, L1_gnn_dec_b0, L1_gnn_dec_W1, L1_gnn_dec_b1, L1_gnn_dec_W2, L1_gnn_dec_b2), axis=-1)
    x = _layernorm(x + _L2_gnn_ref(x, edge_weight1, L2_gnn_W, L2_gnn_b, src, dst), axis=-1)
    x = _layernorm(x + _L3_gnn_ref(x, edge_attr_13, src, dst, L3_gnn_fnet_w1, L3_gnn_fnet_b1, L3_gnn_fnet_w2, L3_gnn_fnet_b2, L3_gnn_gru_w_ih, L3_gnn_gru_w_hh, L3_gnn_gru_b_ih, L3_gnn_gru_b_hh), axis=-1)
    return x

_drawn_inputs = setup_inputs


def setup_inputs(seed=0):
    import zlib

    import numpy as np

    out = dict(_drawn_inputs(seed))
    spreads = {'L1_gnn_enc_b0': (0.0, 2.0),
     'L1_gnn_enc_b1': (0.0, 0.8),
     'L1_gnn_enc_b2': (0.0, 0.8),
     'L1_gnn_lat_b0': (0.0, 0.8),
     'L1_gnn_lat_b1': (0.0, 0.8),
     'L1_gnn_dfc_b0': (0.0, 0.471),
     'L1_gnn_dfc_b1': (0.0, 0.8),
     'L1_gnn_dec_b0': (0.0, 0.1),
     'L1_gnn_dec_b1': (0.0, 0.1),
     'L1_gnn_dec_b2': (0.0, 0.1),
     'L3_gnn_fnet_b1': (0.0, 0.8),
     'L3_gnn_fnet_b2': (0.0, 0.1),
     'L3_gnn_gru_b_ih': (0.0, 0.1),
     'L3_gnn_gru_b_hh': (0.0, 0.334)}
    factors = {'edge_attr_13': 4.383, 'L2_gnn_b': 7.373, 'L3_gnn_fnet_w1': 4.169}
    for name, (base, spread) in spreads.items():
        noise = np.random.default_rng([zlib.crc32(name.encode()), seed]).standard_normal(out[name].shape)
        drawn = base * np.exp(spread * noise) if base else spread * noise
        out[name] = jnp.asarray(drawn.astype(out[name].dtype))
    for name, factor in factors.items():
        out[name] = (out[name] * factor).astype(out[name].dtype)
    return out
```

```python
import concourse.bass as bass
from concourse import mybir
from contextlib import ExitStack
import numpy as np

N = 6250
E = 206250
P = 128
HT = 8
SL = 4
IT = -(-E // (P * SL * HT))
NB = IT * SL
T = NB * HT
HE = HT * P
CH = 512
NC = -(-N // CH)
NP = NC * CH
NTAB = HT
FAR = 1 << 20
BIG = 3.0e38
EPS = 1e-5
SLOPE = 0.01

WEIGHTS = [
    ("ident", (P, P)), ("iota", (P, P)), ("tri", (P, P)), ("ones", (P, P)), ("mean16", (16, 16)),
    ("dummy", (P, 1)), ("rep_i", (16, 256)), ("rep_h", (16, 256)), ("sum_i", (P, 16)),
    ("msg_tp", (16, P)), ("msg_lin", (16, 16)), ("upd_tp", (P, 32)), ("upd_lin", (16, 16)),
    ("enc_W0", (16, 64)), ("enc_b0", (64, 1)), ("enc_W1", (64, 128)), ("enc_b1", (128, 1)),
    ("enc_W2", (128, 64)), ("enc_b2", (64, 1)), ("lat_W0", (64, 32)), ("lat_b0", (32, 1)),
    ("lat_W1", (32, 3)), ("lat_b1", (3, 1)), ("dfc_W0", (3, 32)), ("dfc_b0", (32, 1)),
    ("dfc_W1", (32, 64)), ("dfc_b1", (64, 1)), ("dec_W0", (64, 128)), ("dec_b0", (128, 1)),
    ("dec_W1", (128, 64)), ("dec_b1", (64, 1)), ("dec_W2", (64, 16)), ("dec_b2", (16, 1)),
    ("l2_W", (16, 16)), ("l2_b", (16, 1)), ("f1", (13, 32)), ("fb1", (32, 1)), ("w2b", (33, 256)),
    ("w_ih", (16, 48)), ("w_hh", (16, 48)), ("b_ih", (16, 3)), ("b_hh", (16, 3)),
]


class Steps:

    def __init__(self, sem, per):
        self.sem, self.per = sem, per

    def at(self, k, step):
        return k * self.per + (SL * self.per + step)

    def open(self, eng):
        eng.sem_inc(self.sem, SL * self.per)


def build(nc, a, out):
    fp32 = mybir.dt.float32
    i32 = mybir.dt.int32
    ALU = mybir.AluOpType
    ACT = mybir.ActivationFunctionType
    AX = mybir.AxisListType.X
    ds = bass.ds
    tt, ts, stt = nc.vector.tensor_tensor, nc.vector.tensor_scalar, nc.vector.scalar_tensor_tensor
    act_fn = nc.scalar.activation

    ctx = ExitStack()
    with ctx:
        def sb(name, shape, dt=fp32):
            return ctx.enter_context(nc.sbuf_tensor(name, shape, dt))

        def sem(name):
            return ctx.enter_context(nc.semaphore(name))

        xT = sb("xT", [16, NP])
        acc = sb("acc", [P, NP])
        dinv = sb("dinv", [P, NP])
        invdeg = sb("invdeg", [16, NP])
        hT = dinv[0:16, :]

        w = {name: sb("w_" + name, list(shape)) for name, shape in WEIGHTS}
        base = sb("base", [P, T], i32)
        rel = sb("rel", [P, T])
        rel_last = sb("rel_last", [P, T])
        eps = sb("eps", [P, 1])
        brz = sb("brz", [16, 2])

        idx = [sb(f"idx{h}", [P, HT], i32) for h in range(SL)]
        col = [sb(f"col{h}", [P, HT * 8]) for h in range(2)]
        row = [sb(f"row{h}", [P, HE]) for h in range(2)]
        prev = [sb(f"prev{h}", [16, HE], i32) for h in range(2)]
        scol = [sb(f"scol{h}", [P, HT], i32) for h in range(2)]
        G128 = [sb(f"G{h}", [P, HT, P]) for h in range(2)]
        G = [G128[s // 2][:, :, s % 2 * 64:s % 2 * 64 + 64] for s in range(SL)]
        hot = [sb(f"hot{h}", [P, HT, P]) for h in range(2)]
        same = [sb(f"same{h}", [P, HT, P]) for h in range(2)]
        mpre = [sb(f"mpre{h}", [P, HT, 16]) for h in range(2)]
        msg = [sb(f"msg{h}", [P, HT, 16]) for h in range(2)]
        sc = [sb(f"sc{h}", [P, HT, 16]) for h in range(2)]
        sidx = [sb(f"sidx{h}", [P, HT], i32) for h in range(2)]
        rst = sb("rst", [32, HE])
        wk = sb("wk", [P, 2 * HE])
        tiny = sb("tiny", [P, 4, HT])
        carry = sb("carry", [16, 1])

        gst = sb("gst", [P, CH])
        st1 = sb("st1", [P, CH])
        st2 = sb("st2", [P, CH])
        rzn = sb("rzn", [16, 3, CH])
        tst = sb("tst", [P, 4, P])
        zero = sb("zero", [P, CH])
        ps = ctx.enter_context(nc.psum_tensor("ps", [P, 8, CH], fp32))

        tab128 = nc.dram_tensor("tab128", [NP, P], fp32).ap()
        tab64 = nc.dram_tensor("tab64", [NP, 64], fp32).ap()
        tab16 = nc.dram_tensor("tab16", [NP, 16], fp32).ap()
        scat = [nc.dram_tensor(f"scat{k}", [NP, 16], fp32).ap() for k in range(NTAB)]
        rT = nc.dram_tensor("rT", [32, T * P], fp32).ap()

        NPASS = 10
        PHASES = ["A0", "N0", "N1", "N2", "N3", "N4", "N5", "N6", "N7", "N8", "N9"]
        K = dict(A0=3, N0=29, N1=8, N2=9, N3=18, N4=9, N5=8, N6=16, N7=16, N8=15, N9=22)
        TABLE = dict(A0=tab128, N0=tab16, N1=tab64, N2=tab64, N3=tab64, N4=tab64, N5=tab16, N6=tab16,
                     N7=tab16, N8=tab16, N9=out)
        FEAT = dict(A0=P, N0=16, N1=64, N2=64, N3=64, N4=64, N5=16, N6=16, N7=16, N8=16, N9=16)
        VPER = [18] + [9] * 6 + [14, 13, 13]
        TPER = [2, 1, 2, 1, 1, 1, 1, 3, 8, 8]
        APER = [2, 1, 1, 1, 1, 1, 1, 1, 1, 1]
        LOADS = [3, 0, 1, 0, 0, 0, 0, 3, 1, 1]
        loaded_before = [8 * NB * sum(LOADS[:p]) for p in range(NPASS)]
        NG = [2] + [SL] * (NPASS - 1)

        w_in = sem("w_in")
        ready = sem("ready")
        tbl_out = sem("tbl_out")
        tabs_in = sem("tabs_in")
        loaded = [sem(f"loaded{h}") for h in range(2)]
        indices = [sem(f"indices{s}") for s in range(SL)]
        gathered = [[sem(f"gathered{p}_{s}") for s in range(NG[p])] for p in range(NPASS)]
        gather_go = sem("gather_go")
        pe_go = sem("pe_go")
        dve_go = sem("dve_go")
        retired = sem("retired")
        zeroed = sem("zeroed")
        scattered = [sem(f"scattered{k}") for k in range(NTAB)]
        r_out = sem("r_out")
        vec = [Steps(sem(f"vec{p}"), VPER[p]) for p in range(NPASS)]
        ten = [Steps(sem(f"ten{p}"), TPER[p]) for p in range(NPASS)]
        scl = [Steps(sem(f"scl{p}"), APER[p]) for p in range(NPASS)]
        node = {n: Steps(sem(f"node_{n}"), K[n]) for n in PHASES}

        def tables(n):
            return 16 * NC * n

        def load_count(p, it, b):
            per = 16 * LOADS[p]
            return it * (SL // 2 * per) + (loaded_before[p] + (b // 2 + 1) * per)

        def gather_count(p, it, b):
            per = 16 * HT
            return it * (SL // NG[p] * per) + (b // NG[p] + 1) * per

        def cs(c):
            return ds(c * CH, CH)

        def open_pass(eng, counter, p):
            before = node[PHASES[p]]
            eng.wait_ge(before.sem, before.at(NC - 1, before.per))
            counter.open(eng)

        HOT = 1
        PMUL, PRED, SAME, EARLIER, COUNT, CLIP, TODUMMY, MOVE, SIDX, DEG0 = range(2, 12)
        ADD0 = 2
        MSG, CHANGED, RESET, SCAN, CARRY, END0 = range(2, 8)
        MUL = [2, 3, 6, 9]
        ADDQ = [4, 7, 10, 12]
        WT = [1, 2, 4, 6]
        PR = [3, 5, 7, 8]

        block = ctx.enter_context(nc.Block())

        @block.sync
        def _(sp):
            for name, _ in WEIGHTS:
                sp.dma_start(w[name][:, :], a[name]).then_inc(w_in, 16)
            sp.dma_start(xT[:, :], a["xT"]).then_inc(w_in, 16)
            sp.dma_start(base[:, :], a["base"].to_broadcast([P, T])).then_inc(w_in, 16)
            sp.dma_start(wk[:, 0:T].bitcast(i32), a["dst_p"]).then_inc(w_in, 16)
            sp.dma_start(rel_last[:, :].bitcast(i32), a["dst_n"]).then_inc(w_in, 16)
            sp.wait_ge(ready, 1)
            for k in range(NTAB):
                sp.dma_start(scat[k].rearrange("(p a) f -> p (a f)", p=P),
                             acc[:, 0:NP * 16 // P]).then_inc(zeroed, 16)

            def store_tables(name):
                with sp.Fori(0, NC) as c:
                    sp.wait_ge(node[name].sem, node[name].at(c, K[name]))
                    sp.dma_start(TABLE[name][cs(c), :].rearrange("(j p) f -> p j f", p=P),
                                 tst[:, :, 0:FEAT[name]]).then_inc(tbl_out, 16)

            def edge_loads(p):
                pair = a["dst_g"] if p == 0 else a["src_p"]
                with sp.Fori(0, IT) as it:
                    for b in range(SL):
                        k, h = it * SL + b, b % 2
                        sp.wait_ge(vec[p].sem, vec[p].at(k - SL, VPER[p]))
                        sp.dma_start(idx[b][:, :], pair[:, ds(k * HT, HT)]).then_inc(indices[b], 16)
                        if LOADS[p]:
                            sp.wait_ge(vec[p].sem, vec[p].at(k - 2, VPER[p]))
                        if p == 0:
                            sp.dma_start(scol[h][:, :], a["src_p"][:, ds(k * HT, HT)]).then_inc(loaded[h], 16)
                            sp.dma_start(col[h][:, :], a["ea8"][:, ds(k * HT * 8, HT * 8)]).then_inc(loaded[h], 16)
                            sp.dma_start(row[h][:, :].bitcast(i32),
                                         a["src_r"][0:1, ds(k * HE, HE)].to_broadcast([P, HE])).then_inc(loaded[h], 16)
                        if p == 2:
                            sp.dma_start(row[h][0:13, :], a["ea13"][:, ds(k * HE, HE)]).then_inc(loaded[h], 16)
                        if p == 7:
                            sp.dma_start(col[h][:, 0:HT], a["ew"][:, ds(k * HT, HT)]).then_inc(loaded[h], 16)
                            sp.dma_start(row[h][0:16, :].bitcast(i32),
                                         a["dst_r"][0:1, ds(k * HE, HE)].to_broadcast([16, HE])).then_inc(loaded[h], 16)
                            sp.dma_start(prev[h][:, :],
                                         a["prev_r"][0:1, ds(k * HE, HE)].to_broadcast([16, HE])).then_inc(loaded[h], 16)
                        if p >= 8:
                            sp.dma_start(row[h][0:32, :], rT[:, ds(k * HE, HE)]).then_inc(loaded[h], 16)

            store_tables("A0")
            edge_loads(0)
            for k in range(NTAB):
                sp.wait_ge(scattered[k], 16 * NB)
            with sp.Fori(0, NC) as c:
                sp.wait_ge(node["N0"].sem, node["N0"].at(c - 1, K["N0"]))
                for k in range(NTAB):
                    sp.dma_start(wk[:, k * 64:(k + 1) * 64].rearrange("p (j f) -> p j f", f=16),
                                 scat[k][cs(c), :].rearrange("(j p) f -> p j f", p=P)).then_inc(tabs_in, 16)
                sp.wait_ge(node["N0"].sem, node["N0"].at(c, K["N0"]))
                sp.dma_start(tab16[cs(c), :].rearrange("(j p) f -> p j f", p=P),
                             tst[:, :, 0:16]).then_inc(tbl_out, 16)
            for p in range(1, NPASS):
                edge_loads(p)
                store_tables(PHASES[p + 1])
            sp.wait_ge(tbl_out, tables(len(PHASES)))

        @block.gpsimd
        def _(pool):
            def gathers(p, k, it, b):
                n = NG[p]
                rows = G128 if p == 0 else G
                pool.wait_ge(indices[b], it * 16 + 16 * (IT * p + 1))
                pool.wait_ge(vec[p].sem, vec[p].at(k - n, VPER[p]))
                pool.sem_inc(gather_go, 1)
                for u in range(HT):
                    pool.indirect_dma_start(
                        rows[b % n][:, u, 0:FEAT[PHASES[p]]], None, TABLE[PHASES[p]],
                        bass.IndirectOffsetOnAxis(ap=idx[b][:, u:u + 1], axis=0)).then_inc(gathered[p][b % n], 16)

            def scatters(k, h, first=False):
                pool.wait_ge(vec[0].sem, vec[0].at(k, SIDX))
                pool.wait_ge(scl[0].sem, scl[0].at(k, 2))
                if first:
                    pool.wait_ge(zeroed, 16 * NTAB)
                else:
                    for u in range(NTAB):
                        pool.wait_ge(scattered[u], k * 16)
                pool.sem_inc(retired, 1)
                for u in range(HT):
                    pool.indirect_dma_start(
                        scat[u], bass.IndirectOffsetOnAxis(ap=sidx[h][:, u:u + 1], axis=0),
                        sc[h][:, u, :], None, compute_op=ALU.add).then_inc(scattered[u], 16)

            pool.sem_inc(retired, 1)
            pool.wait_ge(tbl_out, tables(1))
            gathers(0, 0, 0, 0)
            gathers(0, 1, 0, 1)
            scatters(0, 0, first=True)
            gathers(0, 2, 0, 2)
            scatters(1, 1)
            gathers(0, 3, 0, 3)
            scatters(2, 0)
            with pool.Fori(1, IT) as it:
                for b in range(SL):
                    gathers(0, it * SL + b, it, b)
                    scatters(it * SL + (b - 1), (b - 1) % 2)
            scatters(NB - 1, 1)
            for p in range(1, NPASS):
                pool.wait_ge(tbl_out, tables(p + 1))
                with pool.Fori(0, IT) as it:
                    for b in range(SL):
                        gathers(p, it * SL + b, it, b)

        @block.tensor
        def _(pe):
            mm = nc.tensor.matmul

            def windows(p, k, h, rows, F, step):
                pe.wait_ge(vec[p].sem, vec[p].at(k, HOT))
                pe.wait_ge(vec[p].sem, vec[p].at(k - 2, VPER[p]))
                for u in range(HT):
                    last = mm(ps[0:F, 2 * h + u // 4, (u % 4) * P:(u % 4 + 1) * P],
                              rows(u), hot[h][:, u, :], start=True, stop=True)
                last.then_inc(ten[p].sem, 1)

            def step_wait(n, c, step):
                pe.wait_ge(n.sem, n.at(c, step - 1))
                pe.sem_inc(pe_go, 1)

            def table_rows(n, c, step, F):
                step_wait(n, c, step)
                for j in range(4):
                    last = nc.tensor.transpose(ps[:, 2, j * F:(j + 1) * F], gst[0:F, j * P:(j + 1) * P],
                                               w["ident"][0:F, 0:F])
                last.then_inc(n.sem, 1)

            def one(n, c, step, dst, lhsT, rhs):
                step_wait(n, c, step)
                mm(dst, lhsT, rhs, start=True, stop=True).then_inc(n.sem, 1)

            def layernorm(n, c, s):
                one(n, c, s, ps[0:16, 0, :], w["mean16"][:, :], st2[0:16, :])
                one(n, c, s + 3, ps[0:16, 1, :], w["mean16"][:, :], st1[0:16, :])

            pe.wait_ge(w_in, 16 * (len(WEIGHTS) + 4))
            n = node["A0"]
            with pe.Fori(0, NC) as c:
                step_wait(n, c, 2)
                for j in range(4):
                    last = mm(ps[:, 0, j * P:(j + 1) * P], gst[0:16, j * P:(j + 1) * P], w["msg_tp"][:, :],
                              start=True, stop=True)
                last.then_inc(n.sem, 1)

            open_pass(pe, ten[0], 0)
            with pe.Fori(0, IT) as it:
                for b in range(SL):
                    k, h = it * SL + b, b % 2
                    windows(0, k, h, lambda u: w["ones"][:, :], P, 1)
                    pe.wait_ge(scl[0].sem, scl[0].at(k, 1))
                    pe.wait_ge(vec[0].sem, vec[0].at(k, SAME))
                    for u in range(HT):
                        last = mm(ps[:, 4 + h, u * 16:(u + 1) * 16], same[h][:, u, :], msg[h][:, u, :],
                                  start=True, stop=True)
                    last.then_inc(ten[0].sem, 1)

            n = node["N0"]
            with pe.Fori(0, NC) as c:
                step_wait(n, c, 2)
                for j in range(4):
                    last = nc.tensor.transpose(ps[0:16, 0, j * P:(j + 1) * P], st2[:, j * 16:(j + 1) * 16],
                                               w["ident"][:, :])
                last.then_inc(n.sem, 1)
                one(n, c, 4, ps[0:16, 1, :], w["msg_lin"][:, :], st1[0:16, :])
                step_wait(n, c, 7)
                for r in range(2):
                    mm(ps[:, 2 + r, :], w["rep_i"][:, r * P:(r + 1) * P], gst[0:16, :], start=True, stop=True)
                    last = mm(ps[:, 4 + r, :], w["rep_h"][:, r * P:(r + 1) * P], st1[0:16, :], start=True, stop=True)
                last.then_inc(n.sem, 1)
                step_wait(n, c, 10)
                for r in range(2):
                    last = mm(ps[0:16, 0, :], w["upd_tp"][:, r * 16:(r + 1) * 16],
                              wk[:, HE + r * CH:HE + (r + 1) * CH], start=(r == 0), stop=(r == 1))
                last.then_inc(n.sem, 1)
                one(n, c, 12, ps[0:16, 1, :], w["upd_lin"][:, :], st1[0:16, :])
                layernorm(n, c, 15)
                table_rows(n, c, 28, 16)

            def sum_pass(p, F):
                open_pass(pe, ten[p], p)
                with pe.Fori(0, IT) as it:
                    for b in range(SL):
                        k, h = it * SL + b, b % 2
                        if p == 2:
                            pe.wait_ge(loaded[h], load_count(p, it, b))
                            pe.wait_ge(scl[p].sem, scl[p].at(k - 1, 1))
                            pe.sem_inc(pe_go, 1)
                            for q in range(2):
                                last = mm(ps[0:32, 4 + q, :], w["f1"][:, :], row[h][0:13, q * CH:(q + 1) * CH],
                                          start=True, stop=True)
                            last.then_inc(ten[p].sem, 1)
                        pe.wait_ge(gathered[p][b], gather_count(p, it, b))
                        windows(p, k, h, lambda u, g=G[b]: g[:, u, 0:F], F, TPER[p])

            sum_pass(1, 16)
            n = node["N1"]
            with pe.Fori(0, NC) as c:
                one(n, c, 2, ps[0:64, 0, :], w["enc_W0"][:, :], gst[0:16, :])
                table_rows(n, c, 7, 64)
            sum_pass(2, 64)
            n = node["N2"]
            with pe.Fori(0, NC) as c:
                one(n, c, 2, ps[:, 0, :], w["enc_W1"][:, :], gst[0:64, :])
                one(n, c, 5, ps[0:64, 1, :], w["enc_W2"][:, :], st2[:, :])
                table_rows(n, c, 8, 64)
            sum_pass(3, 64)
            n = node["N3"]
            with pe.Fori(0, NC) as c:
                one(n, c, 4, ps[0:32, 0, :], w["lat_W0"][:, :], st2[0:64, :])
                one(n, c, 7, ps[0:3, 1, :], w["lat_W1"][:, :], st2[0:32, :])
                one(n, c, 9, ps[0:32, 0, :], w["dfc_W0"][:, :], st1[0:3, :])
                one(n, c, 12, ps[0:64, 1, :], w["dfc_W1"][:, :], st2[0:32, :])
                table_rows(n, c, 17, 64)
            sum_pass(4, 64)
            n = node["N4"]
            with pe.Fori(0, NC) as c:
                one(n, c, 2, ps[:, 0, :], w["dec_W0"][:, :], gst[0:64, :])
                one(n, c, 5, ps[0:64, 1, :], w["dec_W1"][:, :], st2[:, :])
                table_rows(n, c, 8, 64)
            sum_pass(5, 64)
            n = node["N5"]
            with pe.Fori(0, NC) as c:
                one(n, c, 4, ps[0:16, 0, :], w["dec_W2"][:, :], st2[0:64, :])
                table_rows(n, c, 7, 16)
            sum_pass(6, 16)
            n = node["N6"]
            with pe.Fori(0, NC) as c:
                layernorm(n, c, 6)
                table_rows(n, c, 15, 16)

            p = 7
            open_pass(pe, ten[p], p)
            with pe.Fori(0, IT) as it:
                for b in range(SL):
                    k, h = it * SL + b, b % 2
                    pe.wait_ge(vec[p].sem, vec[p].at(k, MSG))
                    pe.wait_ge(vec[p].sem, vec[p].at(k - 1, SCAN))
                    for u in range(HT):
                        last = nc.tensor.transpose(ps[0:16, 4 + u // 4, (u % 4) * P:(u % 4 + 1) * P],
                                                   msg[h][:, u, :], w["ident"][:, :])
                    last.then_inc(ten[p].sem, 1)
                    pe.wait_ge(vec[p].sem, vec[p].at(k, SCAN))
                    pe.wait_ge(scl[p].sem, scl[p].at(k - 1, 1))
                    pe.sem_inc(pe_go, 1)
                    for u in range(HT):
                        last = nc.tensor.transpose(ps[:, 6, u * 16:(u + 1) * 16],
                                                   wk[0:16, HE + u * P:HE + (u + 1) * P], w["ident"][0:16, 0:16])
                    last.then_inc(ten[p].sem, 1)
                    pe.wait_ge(scl[p].sem, scl[p].at(k, 1))
                    windows(p, k, h, lambda u: sc[h][:, u, :], 16, 3)
            n = node["N7"]
            with pe.Fori(0, NC) as c:
                one(n, c, 2, ps[0:16, 3, :], w["l2_W"][:, :], gst[0:16, :])
                layernorm(n, c, 5)
                table_rows(n, c, 15, 16)

            pe.wait_ge(ready, 11)
            for p in (8, 9):
                open_pass(pe, ten[p], p)
                with pe.Fori(0, IT) as it:
                    for b in range(SL):
                        k, h = it * SL + b, b % 2

                        def message_weights(q):
                            pe.wait_ge(vec[p].sem, vec[p].at(k - 1, MUL[q + 2]) if q < 2 else vec[p].at(k, MUL[q - 2]))
                            pe.sem_inc(pe_go, 1)
                            for u in (2 * q, 2 * q + 1):
                                last = mm(ps[:, 4 + q % 2, (u % 2) * 256:(u % 2 + 1) * 256],
                                          row[h][0:33, u * P:(u + 1) * P], w["w2b"][:, :], start=True, stop=True)
                            last.then_inc(ten[p].sem, 1)

                        def products(q):
                            pe.wait_ge(vec[p].sem, vec[p].at(k, MUL[q]))
                            pe.wait_ge(vec[p].sem, vec[p].at(k - 1, ADDQ[q] + 1))
                            for u in (2 * q, 2 * q + 1):
                                for r in range(2):
                                    last = mm(ps[:, q, (u % 2) * P:(u % 2 + 1) * P],
                                              wk[:, u * 256 + r * P:u * 256 + (r + 1) * P], hot[h][:, u, :],
                                              start=(r == 0), stop=(r == 1))
                            last.then_inc(ten[p].sem, 1)

                        pe.wait_ge(loaded[h], load_count(p, it, b))
                        message_weights(0)
                        message_weights(1)
                        products(0)
                        message_weights(2)
                        products(1)
                        message_weights(3)
                        products(2)
                        products(3)
                n = node[PHASES[p + 1]]
                with pe.Fori(0, NC) as c:
                    pe.wait_ge(vec[p].sem, vec[p].at(NB - 1, VPER[p]))
                    pe.wait_ge(n.sem, n.at(c, 0))
                    mm(ps[0:16, 7, :], w["sum_i"][:, :], acc[:, cs(c)], start=True, stop=True).then_inc(n.sem, 1)
                    step_wait(n, c, 4)
                    for g in range(2):
                        mm(ps[0:16, 3 + g, :], w["w_ih"][:, g * 16:(g + 1) * 16], gst[0:16, :], start=True, stop=False)
                        mm(ps[0:16, 3 + g, :], w["w_hh"][:, g * 16:(g + 1) * 16], st2[0:16, :], start=False, stop=True)
                    mm(ps[0:16, 6, :], w["w_ih"][:, 32:48], gst[0:16, :], start=True, stop=True)
                    mm(ps[0:16, 5, :], w["w_hh"][:, 32:48], st2[0:16, :], start=True, stop=True).then_inc(n.sem, 1)
                    if p == 8:
                        table_rows(n, c, 14, 16)
                    else:
                        layernorm(n, c, 13)
                        table_rows(n, c, 21, 16)

        @block.scalar
        def _(act):
            def store_rows(n, c, step, F, before):
                act.wait_ge(n.sem, n.at(c, step - 1))
                if before is not None:
                    act.wait_ge(tbl_out, tables(before) + c * 16)
                bank = 0 if F == P else 2
                act_fn(tst[:, :, 0:F], ps[:, bank, 0:4 * F].rearrange("p (j f) -> p j f", f=F),
                       ACT.Copy).then_inc(n.sem, 1)

            def one(n, c, step, dst, src, fn, **kw):
                act.wait_ge(n.sem, n.at(c, step - 1))
                act_fn(dst, src, fn, **kw).then_inc(n.sem, 1)

            def layernorm(n, c, s):
                one(n, c, s + 4, st1[0:16, :], ps[0:16, 1, :], ACT.Sqrt, bias=eps[0:16, :])

            act.wait_ge(w_in, 16 * (len(WEIGHTS) + 4))
            act.wait_ge(ready, 9)
            n = node["A0"]
            store_rows(n, 0, 3, P, None)
            with act.Fori(1, NC) as c:
                store_rows(n, c, 3, P, 0)

            open_pass(act, scl[0], 0)
            with act.Fori(0, IT) as it:
                for b in range(SL):
                    k, h = it * SL + b, b % 2
                    act.wait_ge(vec[0].sem, vec[0].at(k, PRED))
                    act.wait_ge(ten[0].sem, ten[0].at(k - 2, 2))
                    act_fn(msg[h][:, :, :], mpre[h][:, :, :], ACT.Silu, scale=float(1 / np.sqrt(16 * 8))
                           ).then_inc(scl[0].sem, 1)
                    act.wait_ge(ten[0].sem, ten[0].at(k, 2))
                    act.wait_ge(retired, k + 1)
                    act_fn(sc[h][:, :, :], ps[:, 4 + h, 0:P].rearrange("p (u f) -> p u f", f=16),
                           ACT.Copy).then_inc(scl[0].sem, 1)

            n = node["N0"]
            with act.Fori(0, NC) as c:
                one(n, c, 3, st1[0:16, :], ps[0:16, 0, :], ACT.Copy)
                one(n, c, 5, st1[0:16, :], ps[0:16, 1, :], ACT.Copy, scale=0.25)
                one(n, c, 8, wk[:, HE:2 * HE].rearrange("p (r n) -> p r n", r=2), ps[:, 2:4, :], ACT.Copy)
                one(n, c, 11, st1[0:16, :], ps[0:16, 0, :], ACT.Silu, scale=1 / 16.0)
                layernorm(n, c, 15)
                one(n, c, 24, dinv[:, cs(c)], dinv[:, cs(c)], ACT.Sqrt, bias=w["ones"][:, 0:1])
                store_rows(n, c, 29, 16, 1)

            n = node["N1"]
            with act.Fori(0, NC) as c:
                one(n, c, 3, st1[0:64, :], ps[0:64, 0, :], ACT.Identity, bias=w["enc_b0"][:, :])
                store_rows(n, c, 8, 64, 2)
            open_pass(act, scl[2], 2)
            with act.Fori(0, NB) as k:
                act.wait_ge(ten[2].sem, ten[2].at(k, 1))
                act_fn(rst[:, :].rearrange("p (q n) -> p q n", q=2), ps[0:32, 4:6, :], ACT.Relu,
                       bias=w["fb1"][:, :]).then_inc(scl[2].sem, 1)
                act.wait_ge(scl[2].sem, scl[2].at(k, 1))
                act.dma_start(rT[:, ds(k * HE, HE)], rst[:, :]).then_inc(r_out, 16)
                act.wait_ge(r_out, k * 16 + 16)
            n = node["N2"]
            with act.Fori(0, NC) as c:
                one(n, c, 3, st1[:, :], ps[:, 0, :], ACT.Identity, bias=w["enc_b1"][:, :])
                store_rows(n, c, 9, 64, 3)
            n = node["N3"]
            with act.Fori(0, NC) as c:
                one(n, c, 2, st1[0:64, :], gst[0:64, :], ACT.Identity, bias=w["enc_b2"][:, :])
                one(n, c, 5, st1[0:32, :], ps[0:32, 0, :], ACT.Identity, bias=w["lat_b0"][:, :])
                one(n, c, 8, st1[0:3, :], ps[0:3, 1, :], ACT.Identity, bias=w["lat_b1"][:, :])
                one(n, c, 10, st1[0:32, :], ps[0:32, 0, :], ACT.Identity, bias=w["dfc_b0"][:, :])
                one(n, c, 13, st1[0:64, :], ps[0:64, 1, :], ACT.Identity, bias=w["dfc_b1"][:, :])
                store_rows(n, c, 18, 64, 4)
            n = node["N4"]
            with act.Fori(0, NC) as c:
                one(n, c, 3, st1[:, :], ps[:, 0, :], ACT.Identity, bias=w["dec_b0"][:, :])
                store_rows(n, c, 9, 64, 5)
            n = node["N5"]
            with act.Fori(0, NC) as c:
                one(n, c, 2, st1[0:64, :], gst[0:64, :], ACT.Identity, bias=w["dec_b1"][:, :])
                store_rows(n, c, 8, 16, 6)
            n = node["N6"]
            with act.Fori(0, NC) as c:
                one(n, c, 2, st1[0:16, :], gst[0:16, :], ACT.Identity, bias=w["dec_b2"][:, :])
                one(n, c, 4, st1[0:16, :], st2[0:16, :], ACT.Tanh)
                layernorm(n, c, 6)
                store_rows(n, c, 16, 16, 7)

            open_pass(act, scl[7], 7)
            with act.Fori(0, IT) as it:
                for b in range(SL):
                    k, h = it * SL + b, b % 2
                    act.wait_ge(ten[7].sem, ten[7].at(k, 2))
                    act.wait_ge(ten[7].sem, ten[7].at(k - 2, 3))
                    act_fn(sc[h][:, :, :], ps[:, 6, 0:P].rearrange("p (u f) -> p u f", f=16),
                           ACT.Copy).then_inc(scl[7].sem, 1)
            n = node["N7"]
            with act.Fori(0, NC) as c:
                one(n, c, 4, st2[0:16, :], st2[0:16, :], ACT.Identity, bias=w["l2_b"][:, :])
                layernorm(n, c, 5)
                store_rows(n, c, 16, 16, 8)

            for p in (8, 9):
                n = node[PHASES[p + 1]]
                with act.Fori(0, NC) as c:
                    act.wait_ge(n.sem, n.at(c, 4))
                    for g in range(2):
                        act_fn(rzn[:, g, :], ps[0:16, 3 + g, :], ACT.Sigmoid, bias=brz[:, g:g + 1])
                    act_fn(rzn[:, 2, :], ps[0:16, 5, :], ACT.Identity, bias=w["b_hh"][:, 2:3]).then_inc(n.sem, 1)
                    one(n, c, 8, st1[0:16, :], st1[0:16, :], ACT.Tanh, bias=w["b_ih"][:, 2:3])
                    if p == 8:
                        store_rows(n, c, 15, 16, 9)
                    else:
                        layernorm(n, c, 13)
                        store_rows(n, c, 22, 16, 10)

        @block.vector
        def _(dve):
            def one_hot(p, k, h, r):
                dve.wait_ge(ten[p].sem, ten[p].at(k - 2, TPER[p]))
                tt(hot[h][:, :, :], w["iota"][:, :].unsqueeze(1).to_broadcast([P, HT, P]),
                   r[:, ds(k * HT, HT)].unsqueeze(2).to_broadcast([P, HT, P]), ALU.is_equal
                   ).then_inc(vec[p].sem, 1)

            first_node = [dve.alloc_register(f"first_node{u}") for u in range(HT)]

            def load_firsts(k):
                dve.load(first_node, base[0:1, ds(k * HT, HT)])
                return [dve.snap(r, min_val=0, max_val=N) for r in first_node]

            def add_windows(p, k, at, dst, F, first, tiles, window):
                for i, u in enumerate(tiles):
                    v = at[u]
                    dve.wait_ge(vec[p].sem, vec[p].at(k, first + i - 1))
                    tt(dst[0:F, ds(v, P)], dst[0:F, ds(v, P)],
                       window(u), ALU.add).then_inc(vec[p].sem, 1)

            def half_window(h, F):
                return lambda u: ps[0:F, 2 * h + u // 4, (u % 4) * P:(u % 4 + 1) * P]

            def all_added(p):
                dve.wait_ge(vec[p].sem, vec[p].at(NB - 1, VPER[p]))

            def wait(n, c, step):
                dve.wait_ge(n.sem, n.at(c, step - 1))

            def clear(n, c, F):
                ts(acc[0:F, cs(c)], zero[0:F, :], 1.0, None, ALU.mult).then_inc(n.sem, 1)

            def layernorm(n, c, s):
                wait(n, c, s + 1)
                tt(st2[0:16, :], st2[0:16, :], ps[0:16, 0, :], ALU.subtract).then_inc(n.sem, 1)
                wait(n, c, s + 2)
                tt(st1[0:16, :], st2[0:16, :], st2[0:16, :], ALU.mult).then_inc(n.sem, 1)
                wait(n, c, s + 5)
                nc.vector.reciprocal(st1[0:16, :], st1[0:16, :]).then_inc(n.sem, 1)
                wait(n, c, s + 6)
                tt(xT[:, cs(c)], st2[0:16, :], st1[0:16, :], ALU.mult).then_inc(n.sem, 1)

            def leaky(n, c, step, F):
                wait(n, c, step)
                stt(st2[0:F, :], st1[0:F, :], SLOPE, st1[0:F, :], ALU.mult, ALU.max).then_inc(n.sem, 1)

            def scaled(n, c, step, src, F):
                wait(n, c, step)
                tt(gst[0:F, :], src, dinv[0:F, cs(c)], ALU.mult).then_inc(n.sem, 1)

            def keep(n, c, step, F):
                wait(n, c, step)
                ts(acc[0:F, cs(c)], gst[0:F, :], 1.0, None, ALU.mult).then_inc(n.sem, 1)

            nc.vector.memset(acc[:, :], 0.0).then_inc(ready, 1)
            nc.vector.memset(dinv[:, :], 0.0).then_inc(ready, 1)
            nc.vector.memset(eps[:, :], EPS).then_inc(ready, 1)
            nc.vector.memset(carry[:, :], 0.0).then_inc(ready, 1)
            nc.vector.memset(zero[:, :], 0.0).then_inc(ready, 1)
            dve.wait_ge(w_in, 16 * (len(WEIGHTS) + 4))
            tt(brz[:, :], w["b_ih"][:, 0:2], w["b_hh"][:, 0:2], ALU.add).then_inc(ready, 1)
            tt(rel[:, :], wk[:, 0:T].bitcast(i32), base[:, :], ALU.subtract).then_inc(ready, 1)
            tt(rel_last[:, :], wk[:, 0:T].bitcast(i32), rel_last[:, :].bitcast(i32), ALU.is_equal).then_inc(ready, 1)
            dve.wait_ge(ready, 8)
            stt(rel_last[:, :], rel_last[:, :], 4096.0, rel[:, :], ALU.mult, ALU.add).then_inc(ready, 1)
            dve.wait_ge(ready, 9)

            n = node["A0"]
            n.open(dve)
            with dve.Fori(0, NC) as c:
                dve.wait_ge(n.sem, n.at(c, 0))
                ts(gst[0:16, :], xT[:, cs(c)], 1.0, None, ALU.mult).then_inc(n.sem, 1)

            v = vec[0]
            open_pass(dve, v, 0)
            with dve.Fori(0, IT) as it:
                for b in range(SL):
                    k, h = it * SL + b, b % 2
                    at = load_firsts(k)
                    one_hot(0, k, h, rel)
                    dve.wait_ge(gathered[0][b % NG[0]], gather_count(0, it, b))
                    dve.wait_ge(loaded[h], load_count(0, it, b))
                    tt(wk[:, 0:HE].rearrange("p (u h j) -> p u h j", u=HT, h=16),
                       G128[h][:, :, :].rearrange("p u (h j) -> p u h j", j=8),
                       col[h][:, :].rearrange("p (u j) -> p u j", j=8).unsqueeze(2).to_broadcast([P, HT, 16, 8]),
                       ALU.mult).then_inc(v.sem, 1)
                    dve.wait_ge(v.sem, v.at(k, PMUL))
                    dve.wait_ge(scl[0].sem, scl[0].at(k - 2, 1))
                    nc.vector.tensor_reduce(mpre[h][:, :, :].rearrange("p u h -> p (u h)"),
                                            wk[:, 0:HE].rearrange("p (x j) -> p x j", j=8), AX, ALU.add
                                            ).then_inc(v.sem, 1)
                    dve.wait_ge(ten[0].sem, ten[0].at(k - 2, 2))
                    tt(same[h][:, :, :], row[h][:, :].bitcast(i32).rearrange("p (u e) -> p u e", e=P),
                       scol[h][:, :].unsqueeze(2).to_broadcast([P, HT, P]), ALU.is_equal).then_inc(v.sem, 1)
                    dve.wait_ge(v.sem, v.at(k, SAME))
                    tt(wk[:, HE:].rearrange("p (u e) -> p u e", e=P), same[h][:, :, :],
                       w["tri"][:, :].unsqueeze(1).to_broadcast([P, HT, P]), ALU.mult).then_inc(v.sem, 1)
                    dve.wait_ge(v.sem, v.at(k, EARLIER))
                    nc.vector.tensor_reduce(tiny[:, 0, :], wk[:, HE:].rearrange("p (u e) -> p u e", e=P), AX,
                                            ALU.add).then_inc(v.sem, 1)
                    dve.wait_ge(v.sem, v.at(k, COUNT))
                    ts(tiny[:, 1, :], tiny[:, 0, :], 1.0, None, ALU.min).then_inc(v.sem, 1)
                    tt(tiny[:, 2, :], w["dummy"][:, 0:1].to_broadcast([P, HT]), scol[h][:, :],
                       ALU.subtract).then_inc(v.sem, 1)
                    dve.wait_ge(v.sem, v.at(k, TODUMMY))
                    tt(tiny[:, 3, :], tiny[:, 1, :], tiny[:, 2, :], ALU.mult).then_inc(v.sem, 1)
                    dve.wait_ge(v.sem, v.at(k, MOVE))
                    dve.wait_ge(retired, k + 1)
                    tt(sidx[h][:, :], tiny[:, 3, :], scol[h][:, :], ALU.add).then_inc(v.sem, 1)
                    dve.wait_ge(ten[0].sem, ten[0].at(k, 1))
                    add_windows(0, k, at, dinv, P, DEG0, range(HT), half_window(h, P))
            all_added(0)

            n = node["N0"]
            n.open(dve)
            with dve.Fori(0, NC) as c:
                dve.wait_ge(tabs_in, c * (16 * NTAB) + 16 * NTAB)
                dve.wait_ge(n.sem, n.at(c, 0))
                nc.vector.tensor_reduce(st2[:, 0:64], wk[:, 0:64 * NTAB].rearrange("p (k f) -> p f k", k=NTAB), AX,
                                        ALU.add).then_inc(n.sem, 1)
                wait(n, c, 6)
                ts(gst[0:16, :], xT[:, cs(c)], 1.0, None, ALU.mult).then_inc(n.sem, 1)
                wait(n, c, 9)
                tt(wk[:, HE:], wk[:, HE:], ps[:, 4:6, :].rearrange("p r n -> p (r n)"), ALU.mult).then_inc(n.sem, 1)
                wait(n, c, 13)
                stt(st2[0:16, :], ps[0:16, 1, :], 0.25, gst[0:16, :], ALU.mult, ALU.add).then_inc(n.sem, 1)
                wait(n, c, 14)
                tt(st2[0:16, :], st2[0:16, :], gst[0:16, :], ALU.add).then_inc(n.sem, 1)
                layernorm(n, c, 15)
                wait(n, c, 22)
                ts(invdeg[:, cs(c)], dinv[0:16, cs(c)], 1.0, None, ALU.max).then_inc(n.sem, 1)
                wait(n, c, 23)
                dve.sem_inc(dve_go, 1)
                nc.vector.reciprocal(invdeg[:, cs(c)], invdeg[:, cs(c)]).then_inc(n.sem, 1)
                wait(n, c, 25)
                dve.sem_inc(dve_go, 1)
                nc.vector.reciprocal(dinv[:, cs(c)], dinv[:, cs(c)]).then_inc(n.sem, 1)
                scaled(n, c, 26, xT[:, cs(c)], 16)
                keep(n, c, 27, 16)

            def sum_pass(p, F):
                open_pass(dve, vec[p], p)
                with dve.Fori(0, IT) as it:
                    for b in range(SL):
                        k, h = it * SL + b, b % 2
                        at = load_firsts(k)
                        one_hot(p, k, h, rel)
                        dve.wait_ge(ten[p].sem, ten[p].at(k, TPER[p]))
                        add_windows(p, k, at, acc, F, ADD0, range(HT), half_window(h, F))
                all_added(p)

            sum_pass(1, 16)
            n = node["N1"]
            n.open(dve)
            with dve.Fori(0, NC) as c:
                scaled(n, c, 1, acc[0:16, cs(c)], 16)
                leaky(n, c, 4, 64)
                scaled(n, c, 5, st2[0:64, :], 64)
                keep(n, c, 6, 64)
            sum_pass(2, 64)
            for p, name in ((2, "N2"), (4, "N4")):
                n = node[name]
                n.open(dve)
                with dve.Fori(0, NC) as c:
                    scaled(n, c, 1, acc[0:64, cs(c)], 64)
                    leaky(n, c, 4, 128)
                    scaled(n, c, 6, ps[0:64, 1, :], 64)
                    keep(n, c, 7, 64)
                sum_pass(p + 1, 64)
                if name == "N4":
                    break
                n = node["N3"]
                n.open(dve)
                with dve.Fori(0, NC) as c:
                    scaled(n, c, 1, acc[0:64, cs(c)], 64)
                    leaky(n, c, 3, 64)
                    leaky(n, c, 6, 32)
                    leaky(n, c, 11, 32)
                    leaky(n, c, 14, 64)
                    scaled(n, c, 15, st2[0:64, :], 64)
                    keep(n, c, 16, 64)
                sum_pass(4, 64)
            n = node["N5"]
            n.open(dve)
            with dve.Fori(0, NC) as c:
                scaled(n, c, 1, acc[0:64, cs(c)], 64)
                leaky(n, c, 3, 64)
                scaled(n, c, 5, ps[0:16, 0, :], 16)
                keep(n, c, 6, 16)
            sum_pass(6, 16)
            n = node["N6"]
            n.open(dve)
            with dve.Fori(0, NC) as c:
                scaled(n, c, 1, acc[0:16, cs(c)], 16)
                leaky(n, c, 3, 16)
                wait(n, c, 5)
                tt(st2[0:16, :], st1[0:16, :], xT[:, cs(c)], ALU.add).then_inc(n.sem, 1)
                layernorm(n, c, 6)
                wait(n, c, 13)
                ts(gst[0:16, :], xT[:, cs(c)], 1.0, None, ALU.mult).then_inc(n.sem, 1)
                clear(n, c, 16)

            v = vec[7]
            open_pass(dve, v, 7)
            with dve.Fori(0, IT) as it:
                for b in range(SL):
                    k, h = it * SL + b, b % 2
                    at = load_firsts(k)
                    one_hot(7, k, h, rel_last)
                    dve.wait_ge(gathered[7][b % NG[7]], gather_count(7, it, b))
                    dve.wait_ge(loaded[h], load_count(7, it, b))
                    dve.wait_ge(ten[7].sem, ten[7].at(k - 2, 1))
                    tt(msg[h][:, :, :], G[b][:, :, 0:16], col[h][:, 0:HT].unsqueeze(2).to_broadcast([P, HT, 16]),
                       ALU.mult).then_inc(v.sem, 1)
                    tt(wk[0:16, 0:HE], row[h][0:16, :].bitcast(i32), prev[h][:, :], ALU.not_equal).then_inc(v.sem, 1)
                    dve.wait_ge(v.sem, v.at(k, CHANGED))
                    ts(wk[0:16, 0:HE], wk[0:16, 0:HE], -BIG, None, ALU.mult).then_inc(v.sem, 1)
                    dve.wait_ge(v.sem, v.at(k, RESET))
                    dve.wait_ge(ten[7].sem, ten[7].at(k, 1))
                    nc.vector.tensor_tensor_scan(wk[0:16, HE:], wk[0:16, 0:HE],
                                                 ps[0:16, 4:6, :].rearrange("p q n -> p (q n)"),
                                                 carry[:, 0:1], ALU.add, ALU.max).then_inc(v.sem, 1)
                    dve.wait_ge(v.sem, v.at(k, SCAN))
                    nc.vector.tensor_copy(carry[:, :], wk[0:16, 2 * HE - 1:2 * HE]).then_inc(v.sem, 1)
                    dve.wait_ge(ten[7].sem, ten[7].at(k, 3))
                    add_windows(7, k, at, acc, 16, END0, range(HT), half_window(h, 16))
            all_added(7)
            n = node["N7"]
            n.open(dve)
            with dve.Fori(0, NC) as c:
                dve.wait_ge(n.sem, n.at(c, 0))
                ts(gst[0:16, :], acc[0:16, cs(c)], 1.0, None, ALU.mult).then_inc(n.sem, 1)
                wait(n, c, 3)
                tt(st2[0:16, :], ps[0:16, 3, :], xT[:, cs(c)], ALU.add).then_inc(n.sem, 1)
                layernorm(n, c, 5)
                wait(n, c, 12)
                ts(hT[:, cs(c)], xT[:, cs(c)], 1.0, None, ALU.mult).then_inc(n.sem, 1)
                clear(n, c, P)
                ts(gst[0:16, :], xT[:, cs(c)], 1.0, None, ALU.mult).then_inc(n.sem, 1)

            for h in range(2):
                nc.vector.memset(row[h][32:33, :], 1.0).then_inc(ready, 1)
            for p in (8, 9):
                v = vec[p]
                open_pass(dve, v, p)
                with dve.Fori(0, IT) as it:
                    for b in range(SL):
                        k, h = it * SL + b, b % 2
                        at = load_firsts(k)
                        one_hot(p, k, h, rel)

                        def multiply(q):
                            dve.wait_ge(ten[p].sem, ten[p].at(k, WT[q]))
                            dve.wait_ge(ten[p].sem, ten[p].at(k - 1, PR[q]))
                            tt(wk[:, q * 512:(q + 1) * 512].rearrange("p (u i o) -> p u i o", u=2, i=16),
                               ps[:, 4 + q % 2, :].rearrange("p (u i o) -> p u i o", u=2, i=16),
                               G[b][:, 2 * q:2 * q + 2, 0:16].unsqueeze(3).to_broadcast([P, 2, 16, 16]),
                               ALU.mult).then_inc(v.sem, 1)

                        def add_pair(q):
                            dve.wait_ge(ten[p].sem, ten[p].at(k, PR[q]))
                            add_windows(p, k, at, acc, P, ADDQ[q], (2 * q, 2 * q + 1),
                                        lambda u: ps[:, q, (u % 2) * P:(u % 2 + 1) * P])

                        dve.wait_ge(gathered[p][b % NG[p]], gather_count(p, it, b))
                        multiply(0)
                        multiply(1)
                        add_pair(0)
                        multiply(2)
                        add_pair(1)
                        multiply(3)
                        add_pair(2)
                        add_pair(3)
                all_added(p)
                n = node[PHASES[p + 1]]
                n.open(dve)
                with dve.Fori(0, NC) as c:
                    wait(n, c, 2)
                    tt(gst[0:16, :], ps[0:16, 7, :], invdeg[:, cs(c)], ALU.mult).then_inc(n.sem, 1)
                    nc.vector.tensor_copy(st2[0:16, :], hT[:, cs(c)]).then_inc(n.sem, 1)
                    wait(n, c, 6)
                    tt(st1[0:16, :], rzn[:, 0, :], rzn[:, 2, :], ALU.mult).then_inc(n.sem, 1)
                    wait(n, c, 7)
                    tt(st1[0:16, :], st1[0:16, :], ps[0:16, 6, :], ALU.add).then_inc(n.sem, 1)
                    wait(n, c, 9)
                    tt(st2[0:16, :], hT[:, cs(c)], st1[0:16, :], ALU.subtract).then_inc(n.sem, 1)
                    wait(n, c, 10)
                    tt(st2[0:16, :], st2[0:16, :], rzn[:, 1, :], ALU.mult).then_inc(n.sem, 1)
                    wait(n, c, 11)
                    tt(hT[:, cs(c)], st2[0:16, :], st1[0:16, :], ALU.add).then_inc(n.sem, 1)
                    wait(n, c, 12)
                    if p == 8:
                        ts(gst[0:16, :], hT[:, cs(c)], 1.0, None, ALU.mult).then_inc(n.sem, 1)
                        clear(n, c, P)
                    else:
                        tt(st2[0:16, :], hT[:, cs(c)], xT[:, cs(c)], ALU.add).then_inc(n.sem, 1)
                        layernorm(n, c, 13)
                        wait(n, c, 20)
                        ts(gst[0:16, :], xT[:, cs(c)], 1.0, None, ALU.mult).then_inc(n.sem, 1)


def _constants():
    f = np.float32
    i, h = np.arange(256) // 16, np.arange(256) % 16
    return {
        "ident": np.eye(P, dtype=f), "iota": np.tile(np.arange(P, dtype=f), (P, 1)),
        "tri": np.tril(np.ones((P, P), f), -1), "ones": np.ones((P, P), f),
        "mean16": np.full((16, 16), 1 / 16, f), "dummy": (N + np.arange(P, dtype=f))[:, None],
        "rep_i": (np.arange(16)[:, None] == i).astype(f), "rep_h": (np.arange(16)[:, None] == h).astype(f),
        "sum_i": (np.arange(P)[:, None] % 16 == np.arange(16)).astype(f),
    }


def _padded(v, before, after, fill):
    return np.concatenate([np.full(before, fill, v.dtype), v, np.full(after, fill, v.dtype)])


def _layout(x):
    pad = T * P - E
    on_p = lambda v: np.ascontiguousarray(v.reshape(T, P).T)
    rows = lambda v: np.concatenate([v, np.zeros((pad, v.shape[1]), v.dtype)])
    g = {k: np.asarray(v) for k, v in x.items()}
    src, dst = g["src"].astype(np.int32), g["dst"].astype(np.int32)
    far = _padded(dst, 0, pad, FAR)
    a = {
        "xT": np.concatenate([g["x"].T, np.zeros((16, NP - N), np.float32)], 1),
        "src_p": on_p(_padded(src, 0, pad, 0)), "src_r": _padded(src, 0, pad, 0)[None],
        "dst_g": on_p(_padded(dst, 0, pad, 0)), "dst_p": on_p(far), "dst_r": far[None],
        "dst_n": on_p(_padded(dst[1:], 0, pad + 1, FAR)), "prev_r": _padded(dst[:-1], 1, pad, -1)[None],
        "base": _padded(dst[::P], 0, T - len(dst[::P]), 0)[None],
        "ea8": rows(g["edge_attr_8"]).reshape(T, P, 8).transpose(1, 0, 2).reshape(P, T * 8),
        "ea13": rows(g["edge_attr_13"]).T,
        "ew": on_p(_padded(g["edge_weight1"][:, 0], 0, pad, 0)),
        "msg_tp": g["L0_gnn_W_msg_tp"].transpose(0, 2, 1).reshape(16, P), "msg_lin": g["L0_gnn_W_msg_lin"],
        "upd_tp": g["L0_gnn_W_upd_tp"].reshape(2, P, 16).transpose(1, 0, 2).reshape(P, 32),
        "upd_lin": g["L0_gnn_W_upd_lin"],
        "l2_W": g["L2_gnn_W"].T, "l2_b": g["L2_gnn_b"][:, None],
        "f1": g["L3_gnn_fnet_w1"], "fb1": g["L3_gnn_fnet_b1"][:, None],
        "w2b": np.concatenate([g["L3_gnn_fnet_w2"], g["L3_gnn_fnet_b2"][None]]),
        "w_ih": g["L3_gnn_gru_w_ih"].T, "w_hh": g["L3_gnn_gru_w_hh"].T,
        "b_ih": g["L3_gnn_gru_b_ih"].reshape(3, 16).T, "b_hh": g["L3_gnn_gru_b_hh"].reshape(3, 16).T,
    }
    for part in ("enc", "lat", "dfc", "dec"):
        for i in range(3 if part in ("enc", "dec") else 2):
            a[f"{part}_W{i}"] = g[f"L1_gnn_{part}_W{i}"]
            a[f"{part}_b{i}"] = g[f"L1_gnn_{part}_b{i}"][:, None]
    a.update(_constants())
    return {k: np.ascontiguousarray(v) for k, v in a.items()}


def kernel(**inputs):
    import concourse.bacc as _bacc
    from concourse.bass_utils import run_bass_kernel_spmd as _run

    nc = _bacc.Bacc("TRN2", target_bir_lowering=False, num_devices=1)
    arrays = _layout(inputs)
    aps = {k: nc.dram_tensor("in_" + k, v.shape, mybir.dt.from_np(v.dtype), kind="ExternalInput").ap()
           for k, v in arrays.items()}
    out = nc.dram_tensor("out_0", (NP, 16), mybir.dt.float32, kind="ExternalOutput").ap()
    build(nc, aps, out)
    r = _run(nc, [{"in_" + k: v for k, v in arrays.items()}], core_ids=[0])
    return r.results[0]["out_0"][:N]
```

```python
import concourse.bass as bass
from concourse import mybir
from contextlib import ExitStack
import numpy as np

N = 6250
E = 206250
P = 128
HT = 8
SL = 4
IT = -(-E // (P * SL * HT))
NB = IT * SL
T = NB * HT
HE = HT * P
CH = 512
NC = -(-N // CH)
NP = NC * CH
NTAB = HT
FAR = 1 << 20
BIG = 3.0e38
EPS = 1e-5
SLOPE = 0.01

WEIGHTS = [
    ("ident", (P, P)), ("iota", (P, P)), ("tri", (P, P)), ("ones", (P, P)), ("mean16", (16, 16)),
    ("dummy", (P, 1)), ("rep_i", (16, 256)), ("rep_h", (16, 256)),
    ("msg_tp", (16, P)), ("msg_lin", (16, 16)), ("upd_tp", (P, 32)), ("upd_lin", (16, 16)),
    ("enc_W0", (16, 64)), ("enc_b0", (64, 1)), ("enc_W1", (64, 128)), ("enc_b1", (128, 1)),
    ("enc_W2", (128, 64)), ("enc_b2", (64, 1)), ("lat_W0", (64, 32)), ("lat_b0", (32, 1)),
    ("lat_W1", (32, 3)), ("lat_b1", (3, 1)), ("dfc_W0", (3, 32)), ("dfc_b0", (32, 1)),
    ("dfc_W1", (32, 64)), ("dfc_b1", (64, 1)), ("dec_W0", (64, 128)), ("dec_b0", (128, 1)),
    ("dec_W1", (128, 64)), ("dec_b1", (64, 1)), ("dec_W2", (64, 16)), ("dec_b2", (16, 1)),
    ("l2_W", (16, 16)), ("l2_b", (16, 1)), ("f1", (13, 32)), ("fb1", (32, 1)), ("w2b", (33, 256)),
    ("w_ih", (16, 48)), ("w_hh", (16, 48)), ("b_ih", (16, 3)), ("b_hh", (16, 3)),
]


class Steps:

    def __init__(self, sem, per):
        self.sem, self.per = sem, per

    def at(self, k, step):
        return k * self.per + (SL * self.per + step)

    def open(self, eng):
        eng.sem_inc(self.sem, SL * self.per)


def build(nc, a, out):
    fp32 = mybir.dt.float32
    i32 = mybir.dt.int32
    ALU = mybir.AluOpType
    ACT = mybir.ActivationFunctionType
    AX = mybir.AxisListType.X
    ds = bass.ds
    tt, ts, stt = nc.vector.tensor_tensor, nc.vector.tensor_scalar, nc.vector.scalar_tensor_tensor
    act_fn = nc.scalar.activation

    ctx = ExitStack()
    with ctx:
        def sb(name, shape, dt=fp32):
            return ctx.enter_context(nc.sbuf_tensor(name, shape, dt))

        def sem(name):
            return ctx.enter_context(nc.semaphore(name))

        xT = sb("xT", [16, NP])
        acc = sb("acc", [P, NP])
        dinv = sb("dinv", [P, NP])
        invdeg = sb("invdeg", [16, NP])
        hT = dinv[0:16, :]

        w = {name: sb("w_" + name, list(shape)) for name, shape in WEIGHTS}
        base = sb("base", [P, HT + T], i32)
        rel = sb("rel", [P, T])
        rel_last = sb("rel_last", [P, T])
        eps = sb("eps", [P, 1])
        brz = sb("brz", [16, 2])

        idx = [sb(f"idx{h}", [P, HT], i32) for h in range(SL)]
        col = [sb(f"col{h}", [P, HT * 8]) for h in range(2)]
        row = [sb(f"row{h}", [P, HE]) for h in range(2)]
        prev = [sb(f"prev{h}", [16, HE], i32) for h in range(2)]
        scol = [sb(f"scol{h}", [P, HT], i32) for h in range(2)]
        G128 = [sb(f"G{h}", [P, HT, P]) for h in range(2)]
        G = [G128[s // 2][:, :, s % 2 * 64:s % 2 * 64 + 64] for s in range(SL)]
        hot = [sb(f"hot{h}", [P, HT, P]) for h in range(2)]
        same = [sb(f"same{h}", [P, HT, P]) for h in range(2)]
        mpre = [sb(f"mpre{h}", [P, HT, 16]) for h in range(2)]
        msg = [sb(f"msg{h}", [P, HT, 16]) for h in range(2)]
        sc = [sb(f"sc{h}", [P, HT, 16]) for h in range(2)]
        sidx = [sb(f"sidx{h}", [P, HT], i32) for h in range(2)]
        rst = sb("rst", [32, HE])
        wk = sb("wk", [P, 2 * HE])
        tiny = sb("tiny", [P, 4, HT])
        tick = sb("tick", [P, 4])
        carry = sb("carry", [16, 1])

        gst = sb("gst", [P, CH])
        st1 = sb("st1", [P, CH])
        st2 = sb("st2", [P, CH])
        rzn = sb("rzn", [16, 3, CH])
        tst = sb("tst", [P, 4, P])
        zero = sb("zero", [P, CH])
        ps = ctx.enter_context(nc.psum_tensor("ps", [P, 8, CH], fp32))

        tab128 = nc.dram_tensor("tab128", [NP, P], fp32).ap()
        tab64 = nc.dram_tensor("tab64", [NP, 64], fp32).ap()
        tab16 = nc.dram_tensor("tab16", [NP, 16], fp32).ap()
        scat = [nc.dram_tensor(f"scat{k}", [NP, 16], fp32).ap() for k in range(NTAB)]
        rT = nc.dram_tensor("rT", [32, T * P], fp32).ap()

        NPASS = 10
        PHASES = ["A0", "N0", "N1", "N2", "N3", "N4", "N5", "N6", "N7", "N8", "N9"]
        K = dict(A0=3, N0=29, N1=8, N2=9, N3=18, N4=9, N5=8, N6=16, N7=16, N8=14, N9=21)
        TABLE = dict(A0=tab128, N0=tab16, N1=tab64, N2=tab64, N3=tab64, N4=tab64, N5=tab16, N6=tab16,
                     N7=tab16, N8=tab16, N9=out)
        FEAT = dict(A0=P, N0=16, N1=64, N2=64, N3=64, N4=64, N5=16, N6=16, N7=16, N8=16, N9=16)
        USED = [2] + [9] * 6 + [2, 5, 5]
        VPER = [18] + [9] * 6 + [14, 14, 14]
        TPER = [2, 1, 2, 1, 1, 1, 1, 3, 5, 5]
        APER = [2, 1, 1, 1, 1, 1, 1, 1, 1, 1]
        LOADS = [3, 0, 1, 0, 0, 0, 0, 3, 1, 1]
        loaded_before = [8 * NB * sum(LOADS[:p]) for p in range(NPASS)]
        NG = [2] + [SL] * (NPASS - 1)

        w_in = sem("w_in")
        ready = sem("ready")
        tbl_out = sem("tbl_out")
        tabs_in = sem("tabs_in")
        loaded = [sem(f"loaded{h}") for h in range(2)]
        indices = [sem(f"indices{s}") for s in range(SL)]
        gathered = [[sem(f"gathered{p}_{s}") for s in range(NG[p])] for p in range(NPASS)]
        gather_go = sem("gather_go")
        pe_go = sem("pe_go")
        dve_go = sem("dve_go")
        retired = sem("retired")
        zeroed = sem("zeroed")
        scattered = [sem(f"scattered{k}") for k in range(NTAB)]
        r_out = sem("r_out")
        vec = [Steps(sem(f"vec{p}"), VPER[p]) for p in range(NPASS)]
        ten = [Steps(sem(f"ten{p}"), TPER[p]) for p in range(NPASS)]
        scl = [Steps(sem(f"scl{p}"), APER[p]) for p in range(NPASS)]
        node = {n: Steps(sem(f"node_{n}"), K[n]) for n in PHASES}

        def tables(n):
            return 16 * NC * n

        def load_count(p, it, b):
            per = 16 * LOADS[p]
            return it * (SL // 2 * per) + (loaded_before[p] + (b // 2 + 1) * per)

        def gather_count(p, it, b):
            per = 16 * HT
            return it * (SL // NG[p] * per) + (b // NG[p] + 1) * per

        def cs(c):
            return ds(c * CH, CH)

        def open_pass(eng, counter, p):
            before = node[PHASES[p]]
            eng.wait_ge(before.sem, before.at(NC - 1, before.per))
            counter.open(eng)

        HOT = 1
        PMUL, PRED, SAME, EARLIER, COUNT, CLIP, TODUMMY, MOVE, SIDX, DEG0 = range(2, 12)
        ADD0 = 2
        MSG, CHANGED, RESET, END0 = range(2, 6)
        SCAN, CARRY = END0 + HT, END0 + HT + 1
        MUL = [2, 3, 4, 5]
        MESSAGES, END8 = 6, 7
        WT = [1, 2, 3, 4]
        WINDOWS8 = 5

        block = ctx.enter_context(nc.Block())

        @block.sync
        def _(sp):
            for name, _ in WEIGHTS:
                sp.dma_start(w[name][:, :], a[name]).then_inc(w_in, 16)
            sp.dma_start(xT[:, :], a["xT"]).then_inc(w_in, 16)
            sp.dma_start(base[:, :], a["base"].to_broadcast([P, HT + T])).then_inc(w_in, 16)
            sp.dma_start(wk[:, 0:T].bitcast(i32), a["dst_p"]).then_inc(w_in, 16)
            sp.dma_start(rel_last[:, :].bitcast(i32), a["dst_n"]).then_inc(w_in, 16)
            sp.wait_ge(ready, 1)
            for k in range(NTAB):
                sp.dma_start(scat[k].rearrange("(p a) f -> p (a f)", p=P),
                             acc[:, 0:NP * 16 // P]).then_inc(zeroed, 16)

            def store_tables(name):
                with sp.Fori(0, NC) as c:
                    sp.wait_ge(node[name].sem, node[name].at(c, K[name]))
                    sp.dma_start(TABLE[name][cs(c), :].rearrange("(j p) f -> p j f", p=P),
                                 tst[:, :, 0:FEAT[name]]).then_inc(tbl_out, 16)

            def edge_loads(p):
                indices_of = a["dst_g"] if p == 0 else a["src_p"]

                def load_indices(it, b, first):
                    if not first:
                        sp.wait_ge(gathered[p][b % NG[p]], gather_count(p, it - 1, b))
                    sp.dma_start(idx[b][:, :], indices_of[:, ds((it * SL + b) * HT, HT)]).then_inc(indices[b], 16)

                def load_edges(k, h):
                    if LOADS[p]:
                        sp.wait_ge(vec[p].sem, vec[p].at(k - 2, VPER[p]))
                    if p == 0:
                        sp.dma_start(scol[h][:, :], a["src_p"][:, ds(k * HT, HT)]).then_inc(loaded[h], 16)
                        sp.dma_start(col[h][:, :], a["ea8"][:, ds(k * HT * 8, HT * 8)]).then_inc(loaded[h], 16)
                        sp.dma_start(row[h][:, :].bitcast(i32),
                                     a["src_r"][0:1, ds(k * HE, HE)].to_broadcast([P, HE])).then_inc(loaded[h], 16)
                    if p == 2:
                        sp.dma_start(row[h][0:13, :], a["ea13"][:, ds(k * HE, HE)]).then_inc(loaded[h], 16)
                    if p == 7:
                        sp.dma_start(col[h][:, 0:HT], a["ew"][:, ds(k * HT, HT)]).then_inc(loaded[h], 16)
                        sp.dma_start(row[h][0:16, :].bitcast(i32),
                                     a["dst_r"][0:1, ds(k * HE, HE)].to_broadcast([16, HE])).then_inc(loaded[h], 16)
                        sp.dma_start(prev[h][:, :],
                                     a["prev_r"][0:1, ds(k * HE, HE)].to_broadcast([16, HE])).then_inc(loaded[h], 16)
                    if p >= 8:
                        sp.dma_start(row[h][0:32, :], rT[:, ds(k * HE, HE)]).then_inc(loaded[h], 16)

                for b in range(SL):
                    load_indices(0, b, True)
                    if b >= 2:
                        load_edges(b - 2, b % 2)
                with sp.Fori(1, IT) as it:
                    for b in range(SL):
                        load_indices(it, b, False)
                        load_edges(it * SL + (b - 2), b % 2)
                load_edges(NB - 2, 0)
                load_edges(NB - 1, 1)

            store_tables("A0")
            edge_loads(0)
            for k in range(NTAB):
                sp.wait_ge(scattered[k], 16 * NB)
            with sp.Fori(0, NC) as c:
                sp.wait_ge(node["N0"].sem, node["N0"].at(c - 1, K["N0"]))
                for k in range(NTAB):
                    sp.dma_start(wk[:, k * 64:(k + 1) * 64].rearrange("p (j f) -> p j f", f=16),
                                 scat[k][cs(c), :].rearrange("(j p) f -> p j f", p=P)).then_inc(tabs_in, 16)
                sp.wait_ge(node["N0"].sem, node["N0"].at(c, K["N0"]))
                sp.dma_start(tab16[cs(c), :].rearrange("(j p) f -> p j f", p=P),
                             tst[:, :, 0:16]).then_inc(tbl_out, 16)
            for p in range(1, NPASS):
                edge_loads(p)
                store_tables(PHASES[p + 1])
            sp.wait_ge(tbl_out, tables(len(PHASES)))

        @block.gpsimd
        def _(pool):
            def carry_wait(slot):
                return nc.gpsimd.tensor_tensor(tick[:, slot + 2:slot + 3], tick[:, 0:1], tick[:, 1:2], ALU.add)

            nc.gpsimd.memset(tick[:, :], 0.0).then_inc(gather_go, 1)
            pool.wait_ge(gather_go, 1)

            def gathers(p, k, it, b):
                n = NG[p]
                rows = G128 if p == 0 else G
                pool.wait_ge(indices[b], it * 16 + 16 * (IT * p + 1))
                pool.wait_ge(vec[p].sem, vec[p].at(k - n, USED[p]))
                pool.wait_ge(gather_go, k + (p * NB + 1))
                carry_wait(0).then_inc(gather_go, 1)
                for u in range(HT):
                    pool.indirect_dma_start(
                        rows[b % n][:, u, 0:FEAT[PHASES[p]]], None, TABLE[PHASES[p]],
                        bass.IndirectOffsetOnAxis(ap=idx[b][:, u:u + 1], axis=0)).then_inc(gathered[p][b % n], 16)

            def scatters(k, h, first=False):
                pool.wait_ge(vec[0].sem, vec[0].at(k, SIDX))
                pool.wait_ge(scl[0].sem, scl[0].at(k, 2))
                if first:
                    pool.wait_ge(zeroed, 16 * NTAB)
                else:
                    for u in range(NTAB):
                        pool.wait_ge(scattered[u], k * 16)
                pool.wait_ge(retired, k + 1)
                carry_wait(1).then_inc(retired, 1)
                for u in range(HT):
                    pool.indirect_dma_start(
                        scat[u], bass.IndirectOffsetOnAxis(ap=sidx[h][:, u:u + 1], axis=0),
                        sc[h][:, u, :], None, compute_op=ALU.add).then_inc(scattered[u], 16)

            pool.sem_inc(retired, 1)
            pool.wait_ge(tbl_out, tables(1))
            gathers(0, 0, 0, 0)
            gathers(0, 1, 0, 1)
            scatters(0, 0, first=True)
            gathers(0, 2, 0, 2)
            scatters(1, 1)
            gathers(0, 3, 0, 3)
            scatters(2, 0)
            with pool.Fori(1, IT) as it:
                for b in range(SL):
                    gathers(0, it * SL + b, it, b)
                    scatters(it * SL + (b - 1), (b - 1) % 2)
            scatters(NB - 1, 1)
            for p in range(1, NPASS):
                pool.wait_ge(tbl_out, tables(p + 1))
                with pool.Fori(0, IT) as it:
                    for b in range(SL):
                        gathers(p, it * SL + b, it, b)

        @block.tensor
        def _(pe):
            mm = nc.tensor.matmul

            def windows(p, k, h, rows, F):
                pe.wait_ge(vec[p].sem, vec[p].at(k, HOT))
                pe.wait_ge(vec[p].sem, vec[p].at(k - 2, VPER[p]))
                for u in range(HT):
                    last = mm(ps[0:F, 2 * h + u // 4, (u % 4) * P:(u % 4 + 1) * P],
                              rows(u), hot[h][:, u, :], start=True, stop=True)
                last.then_inc(ten[p].sem, 1)

            def step_wait(n, c, step):
                pe.wait_ge(n.sem, n.at(c, step - 1))
                pe.sem_inc(pe_go, 1)

            def table_rows(n, c, step, F):
                step_wait(n, c, step)
                for j in range(4):
                    last = nc.tensor.transpose(ps[:, 2, j * F:(j + 1) * F], gst[0:F, j * P:(j + 1) * P],
                                               w["ident"][0:F, 0:F])
                last.then_inc(n.sem, 1)

            def one(n, c, step, dst, lhsT, rhs):
                step_wait(n, c, step)
                mm(dst, lhsT, rhs, start=True, stop=True).then_inc(n.sem, 1)

            def layernorm(n, c, s):
                one(n, c, s, ps[0:16, 0, :], w["mean16"][:, :], st2[0:16, :])
                one(n, c, s + 3, ps[0:16, 1, :], w["mean16"][:, :], st1[0:16, :])

            pe.wait_ge(w_in, 16 * (len(WEIGHTS) + 4))
            n = node["A0"]
            with pe.Fori(0, NC) as c:
                step_wait(n, c, 2)
                for j in range(4):
                    last = mm(ps[:, 0, j * P:(j + 1) * P], gst[0:16, j * P:(j + 1) * P], w["msg_tp"][:, :],
                              start=True, stop=True)
                last.then_inc(n.sem, 1)

            open_pass(pe, ten[0], 0)
            with pe.Fori(0, IT) as it:
                for b in range(SL):
                    k, h = it * SL + b, b % 2
                    windows(0, k, h, lambda u: w["ones"][:, :], P)
                    pe.wait_ge(scl[0].sem, scl[0].at(k, 1))
                    pe.wait_ge(vec[0].sem, vec[0].at(k, SAME))
                    for u in range(HT):
                        last = mm(ps[:, 4 + h, u * 16:(u + 1) * 16], same[h][:, u, :], msg[h][:, u, :],
                                  start=True, stop=True)
                    last.then_inc(ten[0].sem, 1)

            n = node["N0"]
            with pe.Fori(0, NC) as c:
                step_wait(n, c, 2)
                for j in range(4):
                    last = nc.tensor.transpose(ps[0:16, 0, j * P:(j + 1) * P], st2[:, j * 16:(j + 1) * 16],
                                               w["ident"][:, :])
                last.then_inc(n.sem, 1)
                one(n, c, 4, ps[0:16, 1, :], w["msg_lin"][:, :], st1[0:16, :])
                step_wait(n, c, 7)
                for r in range(2):
                    mm(ps[:, 2 + r, :], w["rep_i"][:, r * P:(r + 1) * P], gst[0:16, :], start=True, stop=True)
                    last = mm(ps[:, 4 + r, :], w["rep_h"][:, r * P:(r + 1) * P], st1[0:16, :], start=True, stop=True)
                last.then_inc(n.sem, 1)
                step_wait(n, c, 10)
                for r in range(2):
                    last = mm(ps[0:16, 0, :], w["upd_tp"][:, r * 16:(r + 1) * 16],
                              wk[:, HE + r * CH:HE + (r + 1) * CH], start=(r == 0), stop=(r == 1))
                last.then_inc(n.sem, 1)
                one(n, c, 12, ps[0:16, 1, :], w["upd_lin"][:, :], st1[0:16, :])
                layernorm(n, c, 15)
                table_rows(n, c, 28, 16)

            def sum_pass(p, F):
                open_pass(pe, ten[p], p)
                with pe.Fori(0, IT) as it:
                    for b in range(SL):
                        k, h = it * SL + b, b % 2
                        if p == 2:
                            pe.wait_ge(loaded[h], load_count(p, it, b))
                            pe.wait_ge(scl[p].sem, scl[p].at(k - 1, 1))
                            pe.sem_inc(pe_go, 1)
                            for q in range(2):
                                last = mm(ps[0:32, 4 + q, :], w["f1"][:, :], row[h][0:13, q * CH:(q + 1) * CH],
                                          start=True, stop=True)
                            last.then_inc(ten[p].sem, 1)
                        pe.wait_ge(gathered[p][b], gather_count(p, it, b))
                        windows(p, k, h, lambda u, g=G[b]: g[:, u, 0:F], F)

            sum_pass(1, 16)
            n = node["N1"]
            with pe.Fori(0, NC) as c:
                one(n, c, 2, ps[0:64, 0, :], w["enc_W0"][:, :], gst[0:16, :])
                table_rows(n, c, 7, 64)
            sum_pass(2, 64)
            n = node["N2"]
            with pe.Fori(0, NC) as c:
                one(n, c, 2, ps[:, 0, :], w["enc_W1"][:, :], gst[0:64, :])
                one(n, c, 5, ps[0:64, 1, :], w["enc_W2"][:, :], st2[:, :])
                table_rows(n, c, 8, 64)
            sum_pass(3, 64)
            n = node["N3"]
            with pe.Fori(0, NC) as c:
                one(n, c, 4, ps[0:32, 0, :], w["lat_W0"][:, :], st2[0:64, :])
                one(n, c, 7, ps[0:3, 1, :], w["lat_W1"][:, :], st2[0:32, :])
                one(n, c, 9, ps[0:32, 0, :], w["dfc_W0"][:, :], st1[0:3, :])
                one(n, c, 12, ps[0:64, 1, :], w["dfc_W1"][:, :], st2[0:32, :])
                table_rows(n, c, 17, 64)
            sum_pass(4, 64)
            n = node["N4"]
            with pe.Fori(0, NC) as c:
                one(n, c, 2, ps[:, 0, :], w["dec_W0"][:, :], gst[0:64, :])
                one(n, c, 5, ps[0:64, 1, :], w["dec_W1"][:, :], st2[:, :])
                table_rows(n, c, 8, 64)
            sum_pass(5, 64)
            n = node["N5"]
            with pe.Fori(0, NC) as c:
                one(n, c, 4, ps[0:16, 0, :], w["dec_W2"][:, :], st2[0:64, :])
                table_rows(n, c, 7, 16)
            sum_pass(6, 16)
            n = node["N6"]
            with pe.Fori(0, NC) as c:
                layernorm(n, c, 6)
                table_rows(n, c, 15, 16)

            pe.wait_ge(ready, 10)
            p = 7
            open_pass(pe, ten[p], p)
            with pe.Fori(0, IT) as it:
                for b in range(SL):
                    k, h = it * SL + b, b % 2
                    pe.wait_ge(vec[p].sem, vec[p].at(k, MSG))
                    pe.wait_ge(vec[p].sem, vec[p].at(k - 1, SCAN))
                    for u in range(HT):
                        last = nc.tensor.transpose(ps[0:16, 4 + u // 4, (u % 4) * P:(u % 4 + 1) * P],
                                                   msg[h][:, u, :], w["ident"][:, :])
                    last.then_inc(ten[p].sem, 1)
                    pe.wait_ge(scl[p].sem, scl[p].at(k - 1, 1))
                    windows(p, k - 1, 1 - h, lambda u: sc[1 - h][:, u, :], 16)
                    pe.wait_ge(vec[p].sem, vec[p].at(k, SCAN))
                    pe.sem_inc(pe_go, 1)
                    for u in range(HT):
                        last = nc.tensor.transpose(ps[:, 6, u * 16:(u + 1) * 16],
                                                   wk[0:16, HE + u * P:HE + (u + 1) * P], w["ident"][0:16, 0:16])
                    last.then_inc(ten[p].sem, 1)
            pe.wait_ge(scl[p].sem, scl[p].at(NB - 1, 1))
            windows(p, NB - 1, 1, lambda u: sc[1][:, u, :], 16)
            n = node["N7"]
            with pe.Fori(0, NC) as c:
                one(n, c, 2, ps[0:16, 3, :], w["l2_W"][:, :], gst[0:16, :])
                layernorm(n, c, 5)
                table_rows(n, c, 15, 16)

            pe.wait_ge(ready, 12)
            for p in (8, 9):
                open_pass(pe, ten[p], p)
                with pe.Fori(0, IT) as it:
                    for b in range(SL):
                        k, h = it * SL + b, b % 2

                        pe.wait_ge(loaded[h], load_count(p, it, b))
                        for q in range(4):
                            pe.wait_ge(vec[p].sem, vec[p].at(k - 1, MUL[q]))
                            pe.sem_inc(pe_go, 1)
                            for u in (2 * q, 2 * q + 1):
                                last = mm(ps[:, 4 + q, (u % 2) * 256:(u % 2 + 1) * 256],
                                          row[h][0:33, u * P:(u + 1) * P], w["w2b"][:, :], start=True, stop=True)
                            last.then_inc(ten[p].sem, 1)
                        pe.wait_ge(vec[p].sem, vec[p].at(k - 1, MESSAGES))
                        windows(p, k - 1, 1 - h, lambda u: msg[1 - h][:, u, :], 16)
                pe.wait_ge(vec[p].sem, vec[p].at(NB - 1, MESSAGES))
                windows(p, NB - 1, 1, lambda u: msg[1][:, u, :], 16)
                n = node[PHASES[p + 1]]
                with pe.Fori(0, NC) as c:
                    step_wait(n, c, 3)
                    for g in range(2):
                        mm(ps[0:16, 3 + g, :], w["w_ih"][:, g * 16:(g + 1) * 16], gst[0:16, :], start=True, stop=False)
                        mm(ps[0:16, 3 + g, :], w["w_hh"][:, g * 16:(g + 1) * 16], st2[0:16, :], start=False, stop=True)
                    mm(ps[0:16, 6, :], w["w_ih"][:, 32:48], gst[0:16, :], start=True, stop=True)
                    mm(ps[0:16, 5, :], w["w_hh"][:, 32:48], st2[0:16, :], start=True, stop=True).then_inc(n.sem, 1)
                    if p == 8:
                        table_rows(n, c, 13, 16)
                    else:
                        layernorm(n, c, 12)
                        table_rows(n, c, 20, 16)

        @block.scalar
        def _(act):
            def store_rows(n, c, step, F, before):
                act.wait_ge(n.sem, n.at(c, step - 1))
                if before is not None:
                    act.wait_ge(tbl_out, tables(before) + c * 16)
                bank = 0 if F == P else 2
                act_fn(tst[:, :, 0:F], ps[:, bank, 0:4 * F].rearrange("p (j f) -> p j f", f=F),
                       ACT.Copy).then_inc(n.sem, 1)

            def one(n, c, step, dst, src, fn, **kw):
                act.wait_ge(n.sem, n.at(c, step - 1))
                act_fn(dst, src, fn, **kw).then_inc(n.sem, 1)

            def layernorm(n, c, s):
                one(n, c, s + 4, st1[0:16, :], ps[0:16, 1, :], ACT.Sqrt, bias=eps[0:16, :])

            act.wait_ge(w_in, 16 * (len(WEIGHTS) + 4))
            act.wait_ge(ready, 9)
            n = node["A0"]
            store_rows(n, 0, 3, P, None)
            with act.Fori(1, NC) as c:
                store_rows(n, c, 3, P, 0)

            open_pass(act, scl[0], 0)
            with act.Fori(0, IT) as it:
                for b in range(SL):
                    k, h = it * SL + b, b % 2
                    act.wait_ge(vec[0].sem, vec[0].at(k, PRED))
                    act.wait_ge(ten[0].sem, ten[0].at(k - 2, 2))
                    act_fn(msg[h][:, :, :], mpre[h][:, :, :], ACT.Silu, scale=float(1 / np.sqrt(16 * 8))
                           ).then_inc(scl[0].sem, 1)
                    act.wait_ge(ten[0].sem, ten[0].at(k, 2))
                    act.wait_ge(retired, k + 1)
                    act_fn(sc[h][:, :, :], ps[:, 4 + h, 0:P].rearrange("p (u f) -> p u f", f=16),
                           ACT.Copy).then_inc(scl[0].sem, 1)

            n = node["N0"]
            with act.Fori(0, NC) as c:
                one(n, c, 3, st1[0:16, :], ps[0:16, 0, :], ACT.Copy)
                one(n, c, 5, st1[0:16, :], ps[0:16, 1, :], ACT.Copy, scale=0.25)
                one(n, c, 8, wk[:, HE:2 * HE].rearrange("p (r n) -> p r n", r=2), ps[:, 2:4, :], ACT.Copy)
                one(n, c, 11, st1[0:16, :], ps[0:16, 0, :], ACT.Silu, scale=1 / 16.0)
                layernorm(n, c, 15)
                one(n, c, 24, dinv[:, cs(c)], dinv[:, cs(c)], ACT.Sqrt, bias=w["ones"][:, 0:1])
                store_rows(n, c, 29, 16, 1)

            n = node["N1"]
            with act.Fori(0, NC) as c:
                one(n, c, 3, st1[0:64, :], ps[0:64, 0, :], ACT.Identity, bias=w["enc_b0"][:, :])
                store_rows(n, c, 8, 64, 2)
            open_pass(act, scl[2], 2)
            with act.Fori(0, NB) as k:
                act.wait_ge(ten[2].sem, ten[2].at(k, 1))
                act_fn(rst[:, :].rearrange("p (q n) -> p q n", q=2), ps[0:32, 4:6, :], ACT.Relu,
                       bias=w["fb1"][:, :]).then_inc(scl[2].sem, 1)
                act.wait_ge(scl[2].sem, scl[2].at(k, 1))
                act.dma_start(rT[:, ds(k * HE, HE)], rst[:, :]).then_inc(r_out, 16)
                act.wait_ge(r_out, k * 16 + 16)
            n = node["N2"]
            with act.Fori(0, NC) as c:
                one(n, c, 3, st1[:, :], ps[:, 0, :], ACT.Identity, bias=w["enc_b1"][:, :])
                store_rows(n, c, 9, 64, 3)
            n = node["N3"]
            with act.Fori(0, NC) as c:
                one(n, c, 2, st1[0:64, :], gst[0:64, :], ACT.Identity, bias=w["enc_b2"][:, :])
                one(n, c, 5, st1[0:32, :], ps[0:32, 0, :], ACT.Identity, bias=w["lat_b0"][:, :])
                one(n, c, 8, st1[0:3, :], ps[0:3, 1, :], ACT.Identity, bias=w["lat_b1"][:, :])
                one(n, c, 10, st1[0:32, :], ps[0:32, 0, :], ACT.Identity, bias=w["dfc_b0"][:, :])
                one(n, c, 13, st1[0:64, :], ps[0:64, 1, :], ACT.Identity, bias=w["dfc_b1"][:, :])
                store_rows(n, c, 18, 64, 4)
            n = node["N4"]
            with act.Fori(0, NC) as c:
                one(n, c, 3, st1[:, :], ps[:, 0, :], ACT.Identity, bias=w["dec_b0"][:, :])
                store_rows(n, c, 9, 64, 5)
            n = node["N5"]
            with act.Fori(0, NC) as c:
                one(n, c, 2, st1[0:64, :], gst[0:64, :], ACT.Identity, bias=w["dec_b1"][:, :])
                store_rows(n, c, 8, 16, 6)
            n = node["N6"]
            with act.Fori(0, NC) as c:
                one(n, c, 2, st1[0:16, :], gst[0:16, :], ACT.Identity, bias=w["dec_b2"][:, :])
                one(n, c, 4, st1[0:16, :], st2[0:16, :], ACT.Tanh)
                layernorm(n, c, 6)
                store_rows(n, c, 16, 16, 7)

            open_pass(act, scl[7], 7)
            with act.Fori(0, IT) as it:
                for b in range(SL):
                    k, h = it * SL + b, b % 2
                    act.wait_ge(ten[7].sem, ten[7].at(k, 3))
                    act.wait_ge(ten[7].sem, ten[7].at(k - 1, 2))
                    act_fn(sc[h][:, :, :], ps[:, 6, 0:P].rearrange("p (u f) -> p u f", f=16),
                           ACT.Copy).then_inc(scl[7].sem, 1)
            n = node["N7"]
            with act.Fori(0, NC) as c:
                one(n, c, 4, st2[0:16, :], st2[0:16, :], ACT.Identity, bias=w["l2_b"][:, :])
                layernorm(n, c, 5)
                store_rows(n, c, 16, 16, 8)

            for p in (8, 9):
                n = node[PHASES[p + 1]]
                with act.Fori(0, NC) as c:
                    act.wait_ge(n.sem, n.at(c, 3))
                    for g in range(2):
                        act_fn(rzn[:, g, :], ps[0:16, 3 + g, :], ACT.Sigmoid, bias=brz[:, g:g + 1])
                    act_fn(rzn[:, 2, :], ps[0:16, 5, :], ACT.Identity, bias=w["b_hh"][:, 2:3]).then_inc(n.sem, 1)
                    one(n, c, 7, st1[0:16, :], st1[0:16, :], ACT.Tanh, bias=w["b_ih"][:, 2:3])
                    if p == 8:
                        store_rows(n, c, 14, 16, 9)
                    else:
                        layernorm(n, c, 12)
                        store_rows(n, c, 21, 16, 10)

        @block.vector
        def _(dve):
            def one_hot(p, k, h, r):
                dve.wait_ge(ten[p].sem, ten[p].at(k - 1, 2) if p == 7 else ten[p].at(k - 2, TPER[p]))
                tt(hot[h][:, :, :], w["iota"][:, :].unsqueeze(1).to_broadcast([P, HT, P]),
                   r[:, ds(k * HT, HT)].unsqueeze(2).to_broadcast([P, HT, P]), ALU.is_equal
                   ).then_inc(vec[p].sem, 1)

            first_node = [dve.alloc_register(f"first_node{u}") for u in range(HT)]

            def load_firsts(k):
                dve.load(first_node, base[0:1, ds(k * HT + HT, HT)])
                return [dve.snap(r, min_val=0, max_val=N) for r in first_node]

            def add_windows(p, k, at, dst, F, first, tiles, window):
                for i, u in enumerate(tiles):
                    v = at[u]
                    dve.wait_ge(vec[p].sem, vec[p].at(k, first + i - 1))
                    tt(dst[0:F, ds(v, P)], dst[0:F, ds(v, P)],
                       window(u), ALU.add).then_inc(vec[p].sem, 1)

            def half_window(h, F):
                return lambda u: ps[0:F, 2 * h + u // 4, (u % 4) * P:(u % 4 + 1) * P]

            def all_added(p):
                dve.wait_ge(vec[p].sem, vec[p].at(NB - 1, VPER[p]))

            def wait(n, c, step):
                dve.wait_ge(n.sem, n.at(c, step - 1))

            def clear(n, c, F):
                ts(acc[0:F, cs(c)], zero[0:F, :], 1.0, None, ALU.mult).then_inc(n.sem, 1)

            def layernorm(n, c, s):
                wait(n, c, s + 1)
                tt(st2[0:16, :], st2[0:16, :], ps[0:16, 0, :], ALU.subtract).then_inc(n.sem, 1)
                wait(n, c, s + 2)
                tt(st1[0:16, :], st2[0:16, :], st2[0:16, :], ALU.mult).then_inc(n.sem, 1)
                wait(n, c, s + 5)
                nc.vector.reciprocal(st1[0:16, :], st1[0:16, :]).then_inc(n.sem, 1)
                wait(n, c, s + 6)
                tt(xT[:, cs(c)], st2[0:16, :], st1[0:16, :], ALU.mult).then_inc(n.sem, 1)

            def leaky(n, c, step, F):
                wait(n, c, step)
                stt(st2[0:F, :], st1[0:F, :], SLOPE, st1[0:F, :], ALU.mult, ALU.max).then_inc(n.sem, 1)

            def scaled(n, c, step, src, F):
                wait(n, c, step)
                tt(gst[0:F, :], src, dinv[0:F, cs(c)], ALU.mult).then_inc(n.sem, 1)

            def keep(n, c, step, F):
                wait(n, c, step)
                ts(acc[0:F, cs(c)], gst[0:F, :], 1.0, None, ALU.mult).then_inc(n.sem, 1)

            nc.vector.memset(acc[:, :], 0.0).then_inc(ready, 1)
            nc.vector.memset(dinv[:, :], 0.0).then_inc(ready, 1)
            nc.vector.memset(eps[:, :], EPS).then_inc(ready, 1)
            nc.vector.memset(carry[:, :], 0.0).then_inc(ready, 1)
            nc.vector.memset(zero[:, :], 0.0).then_inc(ready, 1)
            dve.wait_ge(w_in, 16 * (len(WEIGHTS) + 4))
            tt(brz[:, :], w["b_ih"][:, 0:2], w["b_hh"][:, 0:2], ALU.add).then_inc(ready, 1)
            tt(rel[:, :], wk[:, 0:T].bitcast(i32), base[:, HT:], ALU.subtract).then_inc(ready, 1)
            tt(rel_last[:, :], wk[:, 0:T].bitcast(i32), rel_last[:, :].bitcast(i32), ALU.is_equal).then_inc(ready, 1)
            dve.wait_ge(ready, 8)
            stt(rel_last[:, :], rel_last[:, :], 4096.0, rel[:, :], ALU.mult, ALU.add).then_inc(ready, 1)
            dve.wait_ge(ready, 9)

            n = node["A0"]
            n.open(dve)
            with dve.Fori(0, NC) as c:
                dve.wait_ge(n.sem, n.at(c, 0))
                ts(gst[0:16, :], xT[:, cs(c)], 1.0, None, ALU.mult).then_inc(n.sem, 1)

            v = vec[0]
            open_pass(dve, v, 0)
            with dve.Fori(0, IT) as it:
                for b in range(SL):
                    k, h = it * SL + b, b % 2
                    at = load_firsts(k)
                    one_hot(0, k, h, rel)
                    dve.wait_ge(gathered[0][b % NG[0]], gather_count(0, it, b))
                    dve.wait_ge(loaded[h], load_count(0, it, b))
                    tt(wk[:, 0:HE].rearrange("p (u h j) -> p u h j", u=HT, h=16),
                       G128[h][:, :, :].rearrange("p u (h j) -> p u h j", j=8),
                       col[h][:, :].rearrange("p (u j) -> p u j", j=8).unsqueeze(2).to_broadcast([P, HT, 16, 8]),
                       ALU.mult).then_inc(v.sem, 1)
                    dve.wait_ge(v.sem, v.at(k, PMUL))
                    dve.wait_ge(scl[0].sem, scl[0].at(k - 2, 1))
                    nc.vector.tensor_reduce(mpre[h][:, :, :].rearrange("p u h -> p (u h)"),
                                            wk[:, 0:HE].rearrange("p (x j) -> p x j", j=8), AX, ALU.add
                                            ).then_inc(v.sem, 1)
                    dve.wait_ge(ten[0].sem, ten[0].at(k - 2, 2))
                    tt(same[h][:, :, :], row[h][:, :].bitcast(i32).rearrange("p (u e) -> p u e", e=P),
                       scol[h][:, :].unsqueeze(2).to_broadcast([P, HT, P]), ALU.is_equal).then_inc(v.sem, 1)
                    dve.wait_ge(v.sem, v.at(k, SAME))
                    tt(wk[:, HE:].rearrange("p (u e) -> p u e", e=P), same[h][:, :, :],
                       w["tri"][:, :].unsqueeze(1).to_broadcast([P, HT, P]), ALU.mult).then_inc(v.sem, 1)
                    dve.wait_ge(v.sem, v.at(k, EARLIER))
                    nc.vector.tensor_reduce(tiny[:, 0, :], wk[:, HE:].rearrange("p (u e) -> p u e", e=P), AX,
                                            ALU.add).then_inc(v.sem, 1)
                    dve.wait_ge(v.sem, v.at(k, COUNT))
                    ts(tiny[:, 1, :], tiny[:, 0, :], 1.0, None, ALU.min).then_inc(v.sem, 1)
                    tt(tiny[:, 2, :], w["dummy"][:, 0:1].to_broadcast([P, HT]), scol[h][:, :],
                       ALU.subtract).then_inc(v.sem, 1)
                    dve.wait_ge(v.sem, v.at(k, TODUMMY))
                    tt(tiny[:, 3, :], tiny[:, 1, :], tiny[:, 2, :], ALU.mult).then_inc(v.sem, 1)
                    dve.wait_ge(v.sem, v.at(k, MOVE))
                    dve.wait_ge(retired, k + 1)
                    tt(sidx[h][:, :], tiny[:, 3, :], scol[h][:, :], ALU.add).then_inc(v.sem, 1)
                    dve.wait_ge(ten[0].sem, ten[0].at(k, 1))
                    add_windows(0, k, at, dinv, P, DEG0, range(HT), half_window(h, P))
            all_added(0)

            n = node["N0"]
            n.open(dve)
            with dve.Fori(0, NC) as c:
                dve.wait_ge(tabs_in, c * (16 * NTAB) + 16 * NTAB)
                dve.wait_ge(n.sem, n.at(c, 0))
                nc.vector.tensor_reduce(st2[:, 0:64], wk[:, 0:64 * NTAB].rearrange("p (k f) -> p f k", k=NTAB), AX,
                                        ALU.add).then_inc(n.sem, 1)
                wait(n, c, 6)
                ts(gst[0:16, :], xT[:, cs(c)], 1.0, None, ALU.mult).then_inc(n.sem, 1)
                wait(n, c, 9)
                tt(wk[:, HE:], wk[:, HE:], ps[:, 4:6, :].rearrange("p r n -> p (r n)"), ALU.mult).then_inc(n.sem, 1)
                wait(n, c, 13)
                stt(st2[0:16, :], ps[0:16, 1, :], 0.25, gst[0:16, :], ALU.mult, ALU.add).then_inc(n.sem, 1)
                wait(n, c, 14)
                tt(st2[0:16, :], st2[0:16, :], gst[0:16, :], ALU.add).then_inc(n.sem, 1)
                layernorm(n, c, 15)
                wait(n, c, 22)
                ts(invdeg[:, cs(c)], dinv[0:16, cs(c)], 1.0, None, ALU.max).then_inc(n.sem, 1)
                wait(n, c, 23)
                dve.sem_inc(dve_go, 1)
                nc.vector.reciprocal(invdeg[:, cs(c)], invdeg[:, cs(c)]).then_inc(n.sem, 1)
                wait(n, c, 25)
                dve.sem_inc(dve_go, 1)
                nc.vector.reciprocal(dinv[:, cs(c)], dinv[:, cs(c)]).then_inc(n.sem, 1)
                scaled(n, c, 26, xT[:, cs(c)], 16)
                keep(n, c, 27, 16)

            def sum_pass(p, F):
                open_pass(dve, vec[p], p)
                with dve.Fori(0, IT) as it:
                    for b in range(SL):
                        k, h = it * SL + b, b % 2
                        at = load_firsts(k)
                        one_hot(p, k, h, rel)
                        dve.wait_ge(ten[p].sem, ten[p].at(k, TPER[p]))
                        add_windows(p, k, at, acc, F, ADD0, range(HT), half_window(h, F))
                all_added(p)

            sum_pass(1, 16)
            n = node["N1"]
            n.open(dve)
            with dve.Fori(0, NC) as c:
                scaled(n, c, 1, acc[0:16, cs(c)], 16)
                leaky(n, c, 4, 64)
                scaled(n, c, 5, st2[0:64, :], 64)
                keep(n, c, 6, 64)
            sum_pass(2, 64)

            def two_layers(name):
                n = node[name]
                n.open(dve)
                with dve.Fori(0, NC) as c:
                    scaled(n, c, 1, acc[0:64, cs(c)], 64)
                    leaky(n, c, 4, 128)
                    scaled(n, c, 6, ps[0:64, 1, :], 64)
                    keep(n, c, 7, 64)

            two_layers("N2")
            sum_pass(3, 64)
            n = node["N3"]
            n.open(dve)
            with dve.Fori(0, NC) as c:
                scaled(n, c, 1, acc[0:64, cs(c)], 64)
                leaky(n, c, 3, 64)
                leaky(n, c, 6, 32)
                leaky(n, c, 11, 32)
                leaky(n, c, 14, 64)
                scaled(n, c, 15, st2[0:64, :], 64)
                keep(n, c, 16, 64)
            sum_pass(4, 64)
            two_layers("N4")
            sum_pass(5, 64)
            n = node["N5"]
            n.open(dve)
            with dve.Fori(0, NC) as c:
                scaled(n, c, 1, acc[0:64, cs(c)], 64)
                leaky(n, c, 3, 64)
                scaled(n, c, 5, ps[0:16, 0, :], 16)
                keep(n, c, 6, 16)
            sum_pass(6, 16)
            n = node["N6"]
            n.open(dve)
            with dve.Fori(0, NC) as c:
                scaled(n, c, 1, acc[0:16, cs(c)], 16)
                leaky(n, c, 3, 16)
                wait(n, c, 5)
                tt(st2[0:16, :], st1[0:16, :], xT[:, cs(c)], ALU.add).then_inc(n.sem, 1)
                layernorm(n, c, 6)
                wait(n, c, 13)
                ts(gst[0:16, :], xT[:, cs(c)], 1.0, None, ALU.mult).then_inc(n.sem, 1)
                clear(n, c, 16)

            ts(sc[1][:, :, :], zero[:, 0:P].rearrange("p (u f) -> p u f", f=16), 1.0, None, ALU.mult).then_inc(ready, 1)
            dve.wait_ge(ready, 10)
            v = vec[7]
            open_pass(dve, v, 7)
            with dve.Fori(0, IT) as it:
                for b in range(SL):
                    k, h = it * SL + b, b % 2
                    at = load_firsts(k - 1)
                    one_hot(7, k, h, rel_last)
                    dve.wait_ge(gathered[7][b], gather_count(7, it, b))
                    dve.wait_ge(loaded[h], load_count(7, it, b))
                    dve.wait_ge(ten[7].sem, ten[7].at(k - 2, 1))
                    tt(msg[h][:, :, :], G[b][:, :, 0:16], col[h][:, 0:HT].unsqueeze(2).to_broadcast([P, HT, 16]),
                       ALU.mult).then_inc(v.sem, 1)
                    tt(wk[0:16, 0:HE], row[h][0:16, :].bitcast(i32), prev[h][:, :], ALU.not_equal).then_inc(v.sem, 1)
                    dve.wait_ge(v.sem, v.at(k, CHANGED))
                    ts(wk[0:16, 0:HE], wk[0:16, 0:HE], -BIG, None, ALU.mult).then_inc(v.sem, 1)
                    dve.wait_ge(ten[7].sem, ten[7].at(k, 2))
                    add_windows(7, k, at, acc, 16, END0, range(HT), half_window(1 - h, 16))
                    dve.wait_ge(ten[7].sem, ten[7].at(k, 1))
                    dve.wait_ge(ten[7].sem, ten[7].at(k - 1, 3))
                    nc.vector.tensor_tensor_scan(wk[0:16, HE:], wk[0:16, 0:HE],
                                                 ps[0:16, 4:6, :].rearrange("p q n -> p (q n)"),
                                                 carry[:, 0:1], ALU.add, ALU.max).then_inc(v.sem, 1)
                    dve.wait_ge(v.sem, v.at(k, SCAN))
                    nc.vector.tensor_copy(carry[:, :], wk[0:16, 2 * HE - 1:2 * HE]).then_inc(v.sem, 1)
            at = load_firsts(NB - 1)
            dve.wait_ge(ten[7].sem, ten[7].at(NB, 1))
            add_windows(7, NB, at, acc, 16, 1, range(HT), half_window(1, 16))
            dve.wait_ge(vec[7].sem, vec[7].at(NB, HT))
            n = node["N7"]
            n.open(dve)
            with dve.Fori(0, NC) as c:
                dve.wait_ge(n.sem, n.at(c, 0))
                ts(gst[0:16, :], acc[0:16, cs(c)], 1.0, None, ALU.mult).then_inc(n.sem, 1)
                wait(n, c, 3)
                tt(st2[0:16, :], ps[0:16, 3, :], xT[:, cs(c)], ALU.add).then_inc(n.sem, 1)
                layernorm(n, c, 5)
                wait(n, c, 12)
                ts(hT[:, cs(c)], xT[:, cs(c)], 1.0, None, ALU.mult).then_inc(n.sem, 1)
                clear(n, c, 16)
                ts(gst[0:16, :], xT[:, cs(c)], 1.0, None, ALU.mult).then_inc(n.sem, 1)

            for h in range(2):
                nc.vector.memset(row[h][32:33, :], 1.0).then_inc(ready, 1)
            for p in (8, 9):
                v = vec[p]
                ts(msg[1][:, :, :], zero[:, 0:P].rearrange("p (u f) -> p u f", f=16), 1.0, None, ALU.mult
                   ).then_inc(ready, 1)
                dve.wait_ge(ready, 13 + p - 8)
                open_pass(dve, v, p)
                with dve.Fori(0, IT) as it:
                    for b in range(SL):
                        k, h = it * SL + b, b % 2
                        at = load_firsts(k - 1)
                        one_hot(p, k, h, rel)
                        dve.wait_ge(gathered[p][b % NG[p]], gather_count(p, it, b))
                        for q in range(4):
                            dve.wait_ge(ten[p].sem, ten[p].at(k, WT[q]))
                            tt(wk[:, q * 512:(q + 1) * 512].rearrange("p (u o i) -> p u o i", u=2, i=16),
                               ps[:, 4 + q, :].rearrange("p (u o i) -> p u o i", u=2, i=16),
                               G[b][:, 2 * q:2 * q + 2, 0:16].unsqueeze(2).to_broadcast([P, 2, 16, 16]),
                               ALU.mult).then_inc(v.sem, 1)
                        dve.wait_ge(v.sem, v.at(k, MUL[3]))
                        nc.vector.tensor_reduce(msg[h][:, :, :].rearrange("p u o -> p (u o)"),
                                                wk[:, :].rearrange("p (x i) -> p x i", i=16), AX, ALU.add
                                                ).then_inc(v.sem, 1)
                        dve.wait_ge(ten[p].sem, ten[p].at(k, WINDOWS8))
                        add_windows(p, k, at, acc, 16, END8, range(HT), half_window(1 - h, 16))
                at = load_firsts(NB - 1)
                dve.wait_ge(ten[p].sem, ten[p].at(NB, 1))
                add_windows(p, NB, at, acc, 16, 1, range(HT), half_window(1, 16))
                dve.wait_ge(v.sem, v.at(NB, HT))
                n = node[PHASES[p + 1]]
                n.open(dve)
                with dve.Fori(0, NC) as c:
                    dve.wait_ge(n.sem, n.at(c, 0))
                    tt(gst[0:16, :], acc[0:16, cs(c)], invdeg[:, cs(c)], ALU.mult).then_inc(n.sem, 1)
                    nc.vector.tensor_copy(st2[0:16, :], hT[:, cs(c)]).then_inc(n.sem, 1)
                    wait(n, c, 5)
                    tt(st1[0:16, :], rzn[:, 0, :], rzn[:, 2, :], ALU.mult).then_inc(n.sem, 1)
                    wait(n, c, 6)
                    tt(st1[0:16, :], st1[0:16, :], ps[0:16, 6, :], ALU.add).then_inc(n.sem, 1)
                    wait(n, c, 8)
                    tt(st2[0:16, :], hT[:, cs(c)], st1[0:16, :], ALU.subtract).then_inc(n.sem, 1)
                    wait(n, c, 9)
                    tt(st2[0:16, :], st2[0:16, :], rzn[:, 1, :], ALU.mult).then_inc(n.sem, 1)
                    wait(n, c, 10)
                    tt(hT[:, cs(c)], st2[0:16, :], st1[0:16, :], ALU.add).then_inc(n.sem, 1)
                    wait(n, c, 11)
                    if p == 8:
                        ts(gst[0:16, :], hT[:, cs(c)], 1.0, None, ALU.mult).then_inc(n.sem, 1)
                        clear(n, c, 16)
                    else:
                        tt(st2[0:16, :], hT[:, cs(c)], xT[:, cs(c)], ALU.add).then_inc(n.sem, 1)
                        layernorm(n, c, 12)
                        wait(n, c, 19)
                        ts(gst[0:16, :], xT[:, cs(c)], 1.0, None, ALU.mult).then_inc(n.sem, 1)


def _constants():
    f = np.float32
    i, h = np.arange(256) // 16, np.arange(256) % 16
    return {
        "ident": np.eye(P, dtype=f), "iota": np.tile(np.arange(P, dtype=f), (P, 1)),
        "tri": np.tril(np.ones((P, P), f), -1), "ones": np.ones((P, P), f),
        "mean16": np.full((16, 16), 1 / 16, f), "dummy": (N + np.arange(P, dtype=f))[:, None],
        "rep_i": (np.arange(16)[:, None] == i).astype(f), "rep_h": (np.arange(16)[:, None] == h).astype(f),
    }


def _padded(v, before, after, fill):
    return np.concatenate([np.full(before, fill, v.dtype), v, np.full(after, fill, v.dtype)])


def _layout(x):
    pad = T * P - E
    on_p = lambda v: np.ascontiguousarray(v.reshape(T, P).T)
    rows = lambda v: np.concatenate([v, np.zeros((pad, v.shape[1]), v.dtype)])
    g = {k: np.asarray(v) for k, v in x.items()}
    src, dst = g["src"].astype(np.int32), g["dst"].astype(np.int32)
    far = _padded(dst, 0, pad, FAR)
    a = {
        "xT": np.concatenate([g["x"].T, np.zeros((16, NP - N), np.float32)], 1),
        "src_p": on_p(_padded(src, 0, pad, 0)), "src_r": _padded(src, 0, pad, 0)[None],
        "dst_g": on_p(_padded(dst, 0, pad, 0)), "dst_p": on_p(far), "dst_r": far[None],
        "dst_n": on_p(_padded(dst[1:], 0, pad + 1, FAR)), "prev_r": _padded(dst[:-1], 1, pad, -1)[None],
        "base": _padded(dst[::P], HT, T - len(dst[::P]), 0)[None],
        "ea8": rows(g["edge_attr_8"]).reshape(T, P, 8).transpose(1, 0, 2).reshape(P, T * 8),
        "ea13": rows(g["edge_attr_13"]).T,
        "ew": on_p(_padded(g["edge_weight1"][:, 0], 0, pad, 0)),
        "msg_tp": g["L0_gnn_W_msg_tp"].transpose(0, 2, 1).reshape(16, P), "msg_lin": g["L0_gnn_W_msg_lin"],
        "upd_tp": g["L0_gnn_W_upd_tp"].reshape(2, P, 16).transpose(1, 0, 2).reshape(P, 32),
        "upd_lin": g["L0_gnn_W_upd_lin"],
        "l2_W": g["L2_gnn_W"].T, "l2_b": g["L2_gnn_b"][:, None],
        "f1": g["L3_gnn_fnet_w1"], "fb1": g["L3_gnn_fnet_b1"][:, None],
        "w2b": np.concatenate([g["L3_gnn_fnet_w2"], g["L3_gnn_fnet_b2"][None]]
                              ).reshape(33, 16, 16).transpose(0, 2, 1).reshape(33, 256),
        "w_ih": g["L3_gnn_gru_w_ih"].T, "w_hh": g["L3_gnn_gru_w_hh"].T,
        "b_ih": g["L3_gnn_gru_b_ih"].reshape(3, 16).T, "b_hh": g["L3_gnn_gru_b_hh"].reshape(3, 16).T,
    }
    for part in ("enc", "lat", "dfc", "dec"):
        for i in range(3 if part in ("enc", "dec") else 2):
            a[f"{part}_W{i}"] = g[f"L1_gnn_{part}_W{i}"]
            a[f"{part}_b{i}"] = g[f"L1_gnn_{part}_b{i}"][:, None]
    a.update(_constants())
    return {k: np.ascontiguousarray(v) for k, v in a.items()}


def kernel(**inputs):
    import concourse.bacc as _bacc
    from concourse.bass_utils import run_bass_kernel_spmd as _run

    nc = _bacc.Bacc("TRN2", target_bir_lowering=False, num_devices=1)
    arrays = _layout(inputs)
    aps = {k: nc.dram_tensor("in_" + k, v.shape, mybir.dt.from_np(v.dtype), kind="ExternalInput").ap()
           for k, v in arrays.items()}
    out = nc.dram_tensor("out_0", (NP, 16), mybir.dt.float32, kind="ExternalOutput").ap()
    build(nc, aps, out)
    r = _run(nc, [{"in_" + k: v for k, v in arrays.items()}], core_ids=[0])
    return r.results[0]["out_0"][:N]
```

```python
import concourse.bass as bass
from concourse import mybir
from contextlib import ExitStack
import numpy as np

N = 6250
E = 206250
P = 128
HT = 8
SL = 4
IT = -(-E // (P * SL * HT))
NB = IT * SL
T = NB * HT
HE = HT * P
CH = 512
NC = -(-N // CH)
NP = NC * CH
NTAB = HT
FAR = 1 << 20
BIG = 3.0e38
EPS = 1e-5
SLOPE = 0.01

WEIGHTS = [
    ("ident", (P, P)), ("iota", (P, P)), ("tri", (P, P)), ("ones", (P, P)), ("mean16", (16, 16)),
    ("dummy", (P, 1)), ("rep_i", (16, 256)), ("rep_h", (16, 256)),
    ("msg_tp", (16, P)), ("msg_lin", (16, 16)), ("upd_tp", (P, 32)), ("upd_lin", (16, 16)),
    ("enc_W0", (16, 64)), ("enc_b0", (64, 1)), ("enc_W1", (64, 128)), ("enc_b1", (128, 1)),
    ("enc_W2", (128, 64)), ("enc_b2", (64, 1)), ("lat_W0", (64, 32)), ("lat_b0", (32, 1)),
    ("lat_W1", (32, 3)), ("lat_b1", (3, 1)), ("dfc_W0", (3, 32)), ("dfc_b0", (32, 1)),
    ("dfc_W1", (32, 64)), ("dfc_b1", (64, 1)), ("dec_W0", (64, 128)), ("dec_b0", (128, 1)),
    ("dec_W1", (128, 64)), ("dec_b1", (64, 1)), ("dec_W2", (64, 16)), ("dec_b2", (16, 1)),
    ("l2_W", (16, 16)), ("l2_b", (16, 1)), ("f1", (13, 32)), ("fb1", (32, 1)), ("w2b", (33, 256)),
    ("w_ih", (16, 48)), ("w_hh", (16, 48)), ("b_ih", (16, 3)), ("b_hh", (16, 3)),
]


class Steps:

    def __init__(self, sem, per):
        self.sem, self.per = sem, per

    def at(self, k, step):
        return k * self.per + (SL * self.per + step)

    def open(self, eng):
        eng.sem_inc(self.sem, SL * self.per)


def build(nc, a, out):
    fp32 = mybir.dt.float32
    bf16 = mybir.dt.bfloat16
    i32 = mybir.dt.int32
    ALU = mybir.AluOpType
    ACT = mybir.ActivationFunctionType
    AX = mybir.AxisListType.X
    ds = bass.ds
    tt, ts, stt = nc.vector.tensor_tensor, nc.vector.tensor_scalar, nc.vector.scalar_tensor_tensor
    act_fn = nc.scalar.activation

    ctx = ExitStack()
    with ctx:
        def sb(name, shape, dt=fp32):
            return ctx.enter_context(nc.sbuf_tensor(name, shape, dt))

        def sem(name):
            return ctx.enter_context(nc.semaphore(name))

        xT = sb("xT", [16, NP])
        acc = sb("acc", [P, NP])
        dinv = sb("dinv", [P, NP])
        invdeg = sb("invdeg", [P, NP])
        hT = dinv[0:16, :]

        w = {name: sb("w_" + name, list(shape)) for name, shape in WEIGHTS}
        base = sb("base", [P, HT + T], i32)
        rel = sb("rel", [P, T + HT])
        rel_last = sb("rel_last", [P, T])
        eps = sb("eps", [P, 1])
        brz = sb("brz", [16, 2])

        idx = [sb(f"idx{j}", [P, 2 * HT], i32) for j in range(SL // 2)]
        col = [sb(f"col{h}", [P, HT * 8]) for h in range(2)]
        row = [sb(f"row{h}", [P, HE]) for h in range(2)]
        prev = [sb(f"prev{h}", [P, HE], i32) for h in range(2)]
        scol = [sb(f"scol{h}", [P, HT], i32) for h in range(2)]
        nodes = [sb(f"nodes{h}", [P, HT, P]) for h in range(2)]
        G = [nodes[s // 2][:, :, s % 2 * 64:s % 2 * 64 + 64] for s in range(SL)]
        hot = [sb(f"hot{h}", [P, HT, P]) for h in range(2)]
        hot16 = [hot[h][:, :, :].bitcast(bf16)[:, :, 0:P] for h in range(2)]
        hotT = prev[0][:, :].bitcast(fp32)
        ident16 = sb("ident16", [P, P], bf16)
        ones16 = sb("ones16", [P, P], bf16)
        same = [sb(f"same{h}", [P, HT, P]) for h in range(2)]
        mpre = [sb(f"mpre{h}", [P, HT, 16]) for h in range(2)]
        msg = [sb(f"msg{h}", [P, HT, 16]) for h in range(2)]
        sc = [sb(f"sc{h}", [P, HT, 16]) for h in range(2)]
        sidx = [sb(f"sidx{h}", [P, HT], i32) for h in range(2)]
        rst = sb("rst", [32, HE])
        wk = sb("wk", [P, 2 * HE])
        tiny = sb("tiny", [P, 4, HT])
        carry = sb("carry", [16, 1])

        gst = sb("gst", [P, CH])
        st1 = sb("st1", [P, CH])
        st2 = sb("st2", [P, CH])
        rzn = sb("rzn", [16, 3, CH])
        tst = sb("tst", [P, 4, P])
        zero = sb("zero", [P, CH])
        ps = ctx.enter_context(nc.psum_tensor("ps", [P, 8, CH], fp32))

        tab128 = nc.dram_tensor("tab128", [NP, P], fp32).ap()
        tab64 = nc.dram_tensor("tab64", [NP, 64], fp32).ap()
        tab16 = nc.dram_tensor("tab16", [NP, 16], fp32).ap()
        scat = [nc.dram_tensor(f"scat{k}", [NP, 16], fp32).ap() for k in range(NTAB)]
        rT = nc.dram_tensor("rT", [32, T * P], fp32).ap()

        NPASS = 10
        PHASES = ["A0", "N0", "N1", "N2", "N3", "N4", "N5", "N6", "N7", "N8", "N9"]
        K = dict(A0=3, N0=30, N1=8, N2=9, N3=18, N4=9, N5=8, N6=16, N7=16, N8=14, N9=21)
        TABLE = dict(A0=tab128, N0=tab16, N1=tab64, N2=tab64, N3=tab64, N4=tab64, N5=tab16, N6=tab16,
                     N7=tab16, N8=tab16, N9=out)
        FEAT = dict(A0=P, N0=16, N1=64, N2=64, N3=64, N4=64, N5=16, N6=16, N7=16, N8=16, N9=16)
        USED = [None] + [9] * 6 + [2, 5, 5]
        VPER = [18] + [9] * 6 + [14, 14, 14]
        TPER = [4, 1, 2, 1, 1, 1, 1, 3, 5, 5]
        APER = [3, 1, 1, 1, 1, 1, 1, 1, 1, 1]
        LOADS = [3 + HT, 0, 1, 0, 0, 0, 0, 3, 1, 1]
        loaded_before = [8 * NB * sum(LOADS[:p]) for p in range(NPASS)]

        w_in = sem("w_in")
        ready = sem("ready")
        tbl_out = sem("tbl_out")
        tabs_in = sem("tabs_in")
        loaded = [sem(f"loaded{h}") for h in range(2)]
        indices = [sem(f"indices{j}") for j in range(SL // 2)]
        gathered = [[sem(f"gathered{p}_{s}") for s in range(SL)] for p in range(NPASS)]
        gather_go = sem("gather_go")
        pe_go = sem("pe_go")
        dve_go = sem("dve_go")
        retired = sem("retired")
        zeroed = sem("zeroed")
        scattered = [sem(f"scattered{k}") for k in range(NTAB)]
        r_out = sem("r_out")
        vec = [Steps(sem(f"vec{p}"), VPER[p]) for p in range(NPASS)]
        ten = [Steps(sem(f"ten{p}"), TPER[p]) for p in range(NPASS)]
        scl = [Steps(sem(f"scl{p}"), APER[p]) for p in range(NPASS)]
        node = {n: Steps(sem(f"node_{n}"), K[n]) for n in PHASES}

        def tables(n):
            return 16 * NC * n

        def load_count(p, it, b):
            per = 16 * LOADS[p]
            return it * (SL // 2 * per) + (loaded_before[p] + (b // 2 + 1) * per)

        def gather_count(it):
            return it * (16 * HT) + 16 * HT

        def cs(c):
            return ds(c * CH, CH)

        def open_pass(eng, counter, p):
            before = node[PHASES[p]]
            eng.wait_ge(before.sem, before.at(NC - 1, before.per))
            counter.open(eng)

        HOT = 1
        SAME, EARLIER, COUNT, CLIP, TODUMMY, MOVE, SIDX, DEG0 = range(2, 10)
        PMUL, PRED = DEG0 + HT, DEG0 + HT + 1
        TURN, DEGREES, EXPAND, SUMS = range(1, 5)
        TURNED, SILU, SUMMED = range(1, 4)
        ADD0 = 2
        MSG, CHANGED, RESET, END0 = range(2, 6)
        SCAN, CARRY = END0 + HT, END0 + HT + 1
        MUL = [2, 3, 4, 5]
        MESSAGES, END8 = 6, 7
        WT = [1, 2, 3, 4]
        WINDOWS8 = 5

        block = ctx.enter_context(nc.Block())

        @block.sync
        def _(sp):
            window_start = [sp.alloc_register(f"window_start{u}") for u in range(HT)]
            for name, _ in WEIGHTS:
                sp.dma_start(w[name][:, :], a[name]).then_inc(w_in, 16)
            sp.dma_start(xT[:, :], a["xT"]).then_inc(w_in, 16)
            sp.dma_start(base[:, :], a["base"].to_broadcast([P, HT + T])).then_inc(w_in, 16)
            sp.dma_start(wk[:, 0:T].bitcast(i32), a["dst_p"]).then_inc(w_in, 16)
            sp.dma_start(rel_last[:, :].bitcast(i32), a["dst_n"]).then_inc(w_in, 16)
            sp.wait_ge(ready, 1)
            for k in range(NTAB):
                sp.dma_start(scat[k].rearrange("(p a) f -> p (a f)", p=P),
                             acc[:, 0:NP * 16 // P]).then_inc(zeroed, 16)

            def store_tables(name):
                with sp.Fori(0, NC) as c:
                    sp.wait_ge(node[name].sem, node[name].at(c, K[name]))
                    sp.dma_start(TABLE[name][cs(c), :].rearrange("(j p) f -> p j f", p=P),
                                 tst[:, :, 0:FEAT[name]]).then_inc(tbl_out, 16)

            def edge_loads(p):
                def load_indices(it, j, first):
                    if not first:
                        for b in (2 * j, 2 * j + 1):
                            sp.wait_ge(gathered[p][b], gather_count(it - 1))
                    sp.dma_start(idx[j][:, :], a["src_p"][:, ds((it * SL + 2 * j) * HT, 2 * HT)]
                                 ).then_inc(indices[j], 16)

                def load_edges(k, h):
                    if LOADS[p]:
                        sp.wait_ge(vec[p].sem, vec[p].at(k - 2, VPER[p]))
                    if p == 0:
                        sp.load(window_start, base[0:1, ds(k * HT + HT, HT)])
                        for u, start in enumerate([sp.snap(x, min_val=0, max_val=N) for x in window_start]):
                            sp.dma_start(nodes[h][:, u, :], tab128[ds(start, P), :]).then_inc(loaded[h], 16)
                        sp.dma_start(scol[h][:, :], a["src_p"][:, ds(k * HT, HT)]).then_inc(loaded[h], 16)
                        sp.dma_start(col[h][:, :], a["ea8"][:, ds(k * HT * 8, HT * 8)]).then_inc(loaded[h], 16)
                        sp.dma_start(row[h][:, :].bitcast(i32),
                                     a["src_r"][0:1, ds(k * HE, HE)].to_broadcast([P, HE])).then_inc(loaded[h], 16)
                    if p == 2:
                        sp.dma_start(row[h][0:13, :], a["ea13"][:, ds(k * HE, HE)]).then_inc(loaded[h], 16)
                    if p == 7:
                        sp.dma_start(col[h][:, 0:HT], a["ew"][:, ds(k * HT, HT)]).then_inc(loaded[h], 16)
                        sp.dma_start(row[h][0:16, :].bitcast(i32),
                                     a["dst_r"][0:1, ds(k * HE, HE)].to_broadcast([16, HE])).then_inc(loaded[h], 16)
                        sp.dma_start(prev[h][0:16, :],
                                     a["prev_r"][0:1, ds(k * HE, HE)].to_broadcast([16, HE])).then_inc(loaded[h], 16)
                    if p >= 8:
                        sp.dma_start(row[h][0:32, :], rT[:, ds(k * HE, HE)]).then_inc(loaded[h], 16)

                if p > 0:
                    load_indices(0, 0, True)
                    load_indices(0, 1, True)
                load_edges(0, 0)
                load_edges(1, 1)
                with sp.Fori(1, IT) as it:
                    for j in range(SL // 2):
                        if p > 0:
                            load_indices(it, j, False)
                        load_edges(it * SL + (2 * j - 2), 0)
                        load_edges(it * SL + (2 * j - 1), 1)
                load_edges(NB - 2, 0)
                load_edges(NB - 1, 1)

            store_tables("A0")
            sp.wait_ge(w_in, 16 * (len(WEIGHTS) + 4))
            sp.wait_ge(tbl_out, tables(1))
            edge_loads(0)
            for k in range(NTAB):
                sp.wait_ge(scattered[k], 16 * NB)
            with sp.Fori(0, NC) as c:
                sp.wait_ge(node["N0"].sem, node["N0"].at(c - 1, K["N0"]))
                for k in range(NTAB):
                    sp.dma_start(wk[:, k * 64:(k + 1) * 64].rearrange("p (j f) -> p j f", f=16),
                                 scat[k][cs(c), :].rearrange("(j p) f -> p j f", p=P)).then_inc(tabs_in, 16)
                sp.wait_ge(node["N0"].sem, node["N0"].at(c, K["N0"]))
                sp.dma_start(tab16[cs(c), :].rearrange("(j p) f -> p j f", p=P),
                             tst[:, :, 0:16]).then_inc(tbl_out, 16)
            for p in range(1, NPASS):
                edge_loads(p)
                store_tables(PHASES[p + 1])
            sp.wait_ge(tbl_out, tables(len(PHASES)))

        @block.gpsimd
        def _(pool):
            def gather_rows(p, b):
                for u in range(HT):
                    pool.indirect_dma_start(
                        G[b][:, u, 0:FEAT[PHASES[p]]], None, TABLE[PHASES[p]],
                        bass.IndirectOffsetOnAxis(ap=idx[b // 2][:, b % 2 * HT + u:b % 2 * HT + u + 1], axis=0)
                    ).then_inc(gathered[p][b], 16)

            def gather_two(p, it, j):
                pool.wait_ge(indices[j], it * 16 + 16 * (IT * (p - 1) + 1))
                pool.wait_ge(vec[p].sem, vec[p].at(it * SL + (2 * j + 1 - SL), USED[p]))
                pool.sem_inc(gather_go, 1)
                gather_rows(p, 2 * j)
                gather_rows(p, 2 * j + 1)

            def scatters(k, h, first=False):
                pool.wait_ge(vec[0].sem, vec[0].at(k, SIDX))
                pool.wait_ge(scl[0].sem, scl[0].at(k, SUMMED))
                if first:
                    pool.wait_ge(zeroed, 16 * NTAB)
                for half in range(2):
                    tiles = range(half * HT // 2, (half + 1) * HT // 2)
                    if not first:
                        for u in tiles:
                            pool.wait_ge(scattered[u], k * 16)
                    pool.sem_inc(retired if half else gather_go, 1)
                    for u in tiles:
                        pool.indirect_dma_start(
                            scat[u], bass.IndirectOffsetOnAxis(ap=sidx[h][:, u:u + 1], axis=0),
                            sc[h][:, u, :], None, compute_op=ALU.add).then_inc(scattered[u], 16)

            pool.sem_inc(retired, 1)
            for k in range(SL):
                scatters(k, k % 2, first=(k == 0))
            with pool.Fori(1, IT) as it:
                for b in range(SL):
                    scatters(it * SL + b, b % 2)
            for p in range(1, NPASS):
                pool.wait_ge(tbl_out, tables(p + 1))
                with pool.Fori(0, IT) as it:
                    gather_two(p, it, 0)
                    gather_two(p, it, 1)

        @block.tensor
        def _(pe):
            mm = nc.tensor.matmul

            def windows(p, k, h, rows, F):
                pe.wait_ge(vec[p].sem, vec[p].at(k if p >= 7 else k - 1, HOT))
                pe.wait_ge(vec[p].sem, vec[p].at(k - 2, VPER[p]))
                for u in range(HT):
                    last = mm(ps[0:F, 2 * h + u // 4, (u % 4) * P:(u % 4 + 1) * P],
                              rows(u), hot[h][:, u, :], start=True, stop=True)
                last.then_inc(ten[p].sem, 1)

            def step_wait(n, c, step):
                pe.wait_ge(n.sem, n.at(c, step - 1))
                pe.sem_inc(pe_go, 1)

            def table_rows(n, c, step, F):
                step_wait(n, c, step)
                for j in range(4):
                    last = nc.tensor.transpose(ps[:, 2, j * F:(j + 1) * F], gst[0:F, j * P:(j + 1) * P],
                                               w["ident"][0:F, 0:F])
                last.then_inc(n.sem, 1)

            def one(n, c, step, dst, lhsT, rhs):
                step_wait(n, c, step)
                mm(dst, lhsT, rhs, start=True, stop=True).then_inc(n.sem, 1)

            def layernorm(n, c, s):
                one(n, c, s, ps[0:16, 0, :], w["mean16"][:, :], st2[0:16, :])
                one(n, c, s + 3, ps[0:16, 1, :], w["mean16"][:, :], st1[0:16, :])

            pe.wait_ge(w_in, 16 * (len(WEIGHTS) + 4))
            n = node["A0"]
            with pe.Fori(0, NC) as c:
                step_wait(n, c, 2)
                for j in range(4):
                    last = mm(ps[:, 0, j * P:(j + 1) * P], gst[0:16, j * P:(j + 1) * P], w["msg_tp"][:, :],
                              start=True, stop=True)
                last.then_inc(n.sem, 1)

            open_pass(pe, ten[0], 0)
            turned = ps[:, 5, :].bitcast(bf16)
            with pe.Fori(0, IT) as it:
                for b in range(SL):
                    k, h = it * SL + b, b % 2
                    pe.wait_ge(vec[0].sem, vec[0].at(k - 1, HOT))
                    pe.wait_ge(scl[0].sem, scl[0].at(k - 1, TURNED))
                    pe.sem_inc(pe_go, 1)
                    for u in range(HT):
                        last = nc.tensor.transpose(turned[:, u * P:(u + 1) * P], hot16[h][:, u, :], ident16[:, :])
                    last.then_inc(ten[0].sem, 1)
                    pe.wait_ge(vec[0].sem, vec[0].at(k - 2, VPER[0]))
                    for u in range(HT):
                        last = mm(ps[:, 2 * h + u // 4, (u % 4) * P:(u % 4 + 1) * P], ones16[:, :], hot16[h][:, u, :],
                                  start=True, stop=True)
                    last.then_inc(ten[0].sem, 1)
                    pe.wait_ge(loaded[h], load_count(0, it, b))
                    pe.wait_ge(vec[0].sem, vec[0].at(k - 1, PMUL))
                    pe.wait_ge(scl[0].sem, scl[0].at(k, TURNED))
                    for u in range(HT):
                        last = mm(ps[:, 6 + u // 4, (u % 4) * P:(u % 4 + 1) * P], hotT[:, u * P:(u + 1) * P],
                                  nodes[h][:, u, :], start=True, stop=True)
                    last.then_inc(ten[0].sem, 1)
                    pe.wait_ge(scl[0].sem, scl[0].at(k - 1, SUMMED))
                    pe.wait_ge(scl[0].sem, scl[0].at(k, SILU))
                    pe.wait_ge(vec[0].sem, vec[0].at(k, SAME))
                    for u in range(HT):
                        last = mm(ps[:, 4, u * 16:(u + 1) * 16], same[h][:, u, :], msg[h][:, u, :],
                                  start=True, stop=True)
                    last.then_inc(ten[0].sem, 1)

            n = node["N0"]
            with pe.Fori(0, NC) as c:
                step_wait(n, c, 2)
                for j in range(4):
                    last = nc.tensor.transpose(ps[0:16, 0, j * P:(j + 1) * P], st2[:, j * 16:(j + 1) * 16],
                                               w["ident"][:, :])
                last.then_inc(n.sem, 1)
                one(n, c, 4, ps[0:16, 1, :], w["msg_lin"][:, :], st1[0:16, :])
                step_wait(n, c, 7)
                for r in range(2):
                    mm(ps[:, 2 + r, :], w["rep_i"][:, r * P:(r + 1) * P], gst[0:16, :], start=True, stop=True)
                    last = mm(ps[:, 4 + r, :], w["rep_h"][:, r * P:(r + 1) * P], st1[0:16, :], start=True, stop=True)
                last.then_inc(n.sem, 1)
                step_wait(n, c, 10)
                for r in range(2):
                    last = mm(ps[0:16, 0, :], w["upd_tp"][:, r * 16:(r + 1) * 16],
                              wk[:, HE + r * CH:HE + (r + 1) * CH], start=(r == 0), stop=(r == 1))
                last.then_inc(n.sem, 1)
                one(n, c, 12, ps[0:16, 1, :], w["upd_lin"][:, :], st1[0:16, :])
                layernorm(n, c, 15)
                table_rows(n, c, 29, 16)

            def sum_pass(p, F):
                open_pass(pe, ten[p], p)
                with pe.Fori(0, IT) as it:
                    for b in range(SL):
                        k, h = it * SL + b, b % 2
                        if p == 2:
                            pe.wait_ge(loaded[h], load_count(p, it, b))
                            pe.wait_ge(scl[p].sem, scl[p].at(k - 1, 1))
                            pe.sem_inc(pe_go, 1)
                            for q in range(2):
                                last = mm(ps[0:32, 4 + q, :], w["f1"][:, :], row[h][0:13, q * CH:(q + 1) * CH],
                                          start=True, stop=True)
                            last.then_inc(ten[p].sem, 1)
                        pe.wait_ge(gathered[p][b], gather_count(it))
                        windows(p, k, h, lambda u, g=G[b]: g[:, u, 0:F], F)

            sum_pass(1, 16)
            n = node["N1"]
            with pe.Fori(0, NC) as c:
                one(n, c, 2, ps[0:64, 0, :], w["enc_W0"][:, :], gst[0:16, :])
                table_rows(n, c, 7, 64)
            sum_pass(2, 64)
            n = node["N2"]
            with pe.Fori(0, NC) as c:
                one(n, c, 2, ps[:, 0, :], w["enc_W1"][:, :], gst[0:64, :])
                one(n, c, 5, ps[0:64, 1, :], w["enc_W2"][:, :], st2[:, :])
                table_rows(n, c, 8, 64)
            sum_pass(3, 64)
            n = node["N3"]
            with pe.Fori(0, NC) as c:
                one(n, c, 4, ps[0:32, 0, :], w["lat_W0"][:, :], st2[0:64, :])
                one(n, c, 7, ps[0:3, 1, :], w["lat_W1"][:, :], st2[0:32, :])
                one(n, c, 9, ps[0:32, 0, :], w["dfc_W0"][:, :], st1[0:3, :])
                one(n, c, 12, ps[0:64, 1, :], w["dfc_W1"][:, :], st2[0:32, :])
                table_rows(n, c, 17, 64)
            sum_pass(4, 64)
            n = node["N4"]
            with pe.Fori(0, NC) as c:
                one(n, c, 2, ps[:, 0, :], w["dec_W0"][:, :], gst[0:64, :])
                one(n, c, 5, ps[0:64, 1, :], w["dec_W1"][:, :], st2[:, :])
                table_rows(n, c, 8, 64)
            sum_pass(5, 64)
            n = node["N5"]
            with pe.Fori(0, NC) as c:
                one(n, c, 4, ps[0:16, 0, :], w["dec_W2"][:, :], st2[0:64, :])
                table_rows(n, c, 7, 16)
            sum_pass(6, 16)
            n = node["N6"]
            with pe.Fori(0, NC) as c:
                layernorm(n, c, 6)
                table_rows(n, c, 15, 16)

            pe.wait_ge(ready, 14)
            p = 7
            open_pass(pe, ten[p], p)
            with pe.Fori(0, IT) as it:
                for b in range(SL):
                    k, h = it * SL + b, b % 2
                    pe.wait_ge(scl[p].sem, scl[p].at(k - 1, 1))
                    windows(p, k - 1, 1 - h, lambda u: sc[1 - h][:, u, :], 16)
                    pe.wait_ge(vec[p].sem, vec[p].at(k, MSG))
                    pe.wait_ge(vec[p].sem, vec[p].at(k - 1, SCAN))
                    for u in range(HT):
                        last = nc.tensor.transpose(ps[0:16, 4 + u // 4, (u % 4) * P:(u % 4 + 1) * P],
                                                   msg[h][:, u, :], w["ident"][:, :])
                    last.then_inc(ten[p].sem, 1)
                    pe.wait_ge(vec[p].sem, vec[p].at(k, SCAN))
                    pe.sem_inc(pe_go, 1)
                    for u in range(HT):
                        last = nc.tensor.transpose(ps[:, 6, u * 16:(u + 1) * 16],
                                                   wk[0:16, HE + u * P:HE + (u + 1) * P], w["ident"][0:16, 0:16])
                    last.then_inc(ten[p].sem, 1)
            pe.wait_ge(scl[p].sem, scl[p].at(NB - 1, 1))
            windows(p, NB - 1, 1, lambda u: sc[1][:, u, :], 16)
            n = node["N7"]
            with pe.Fori(0, NC) as c:
                one(n, c, 2, ps[0:16, 3, :], w["l2_W"][:, :], gst[0:16, :])
                layernorm(n, c, 5)
                table_rows(n, c, 15, 16)

            pe.wait_ge(ready, 16)
            for p in (8, 9):
                open_pass(pe, ten[p], p)
                with pe.Fori(0, IT) as it:
                    for b in range(SL):
                        k, h = it * SL + b, b % 2

                        pe.wait_ge(loaded[h], load_count(p, it, b))
                        for q in range(4):
                            pe.wait_ge(vec[p].sem, vec[p].at(k - 1, MUL[q]))
                            pe.sem_inc(pe_go, 1)
                            for u in (2 * q, 2 * q + 1):
                                last = mm(ps[:, 4 + q, (u % 2) * 256:(u % 2 + 1) * 256],
                                          row[h][0:33, u * P:(u + 1) * P], w["w2b"][:, :], start=True, stop=True)
                            last.then_inc(ten[p].sem, 1)
                        pe.wait_ge(vec[p].sem, vec[p].at(k - 1, MESSAGES))
                        windows(p, k - 1, 1 - h, lambda u: msg[1 - h][:, u, :], 16)
                pe.wait_ge(vec[p].sem, vec[p].at(NB - 1, MESSAGES))
                windows(p, NB - 1, 1, lambda u: msg[1][:, u, :], 16)
                n = node[PHASES[p + 1]]
                with pe.Fori(0, NC) as c:
                    step_wait(n, c, 3)
                    for g in range(2):
                        mm(ps[0:16, 3 + g, :], w["w_ih"][:, g * 16:(g + 1) * 16], gst[0:16, :], start=True, stop=False)
                        mm(ps[0:16, 3 + g, :], w["w_hh"][:, g * 16:(g + 1) * 16], st2[0:16, :], start=False, stop=True)
                    mm(ps[0:16, 6, :], w["w_ih"][:, 32:48], gst[0:16, :], start=True, stop=True)
                    mm(ps[0:16, 5, :], w["w_hh"][:, 32:48], st2[0:16, :], start=True, stop=True).then_inc(n.sem, 1)
                    if p == 8:
                        table_rows(n, c, 13, 16)
                    else:
                        layernorm(n, c, 12)
                        table_rows(n, c, 20, 16)

        @block.scalar
        def _(act):
            def store_rows(n, c, step, F, before):
                act.wait_ge(n.sem, n.at(c, step - 1))
                if before is not None:
                    act.wait_ge(tbl_out, tables(before) + c * 16)
                bank = 0 if F == P else 2
                act_fn(tst[:, :, 0:F], ps[:, bank, 0:4 * F].rearrange("p (j f) -> p j f", f=F),
                       ACT.Copy).then_inc(n.sem, 1)

            def one(n, c, step, dst, src, fn, **kw):
                act.wait_ge(n.sem, n.at(c, step - 1))
                act_fn(dst, src, fn, **kw).then_inc(n.sem, 1)

            def layernorm(n, c, s):
                one(n, c, s + 4, st1[0:16, :], ps[0:16, 1, :], ACT.Sqrt, bias=eps[0:16, :])

            act.wait_ge(w_in, 16 * (len(WEIGHTS) + 4))
            act.wait_ge(ready, 13)
            n = node["A0"]
            store_rows(n, 0, 3, P, None)
            with act.Fori(1, NC) as c:
                store_rows(n, c, 3, P, 0)

            open_pass(act, scl[0], 0)
            with act.Fori(0, IT) as it:
                for b in range(SL):
                    k, h = it * SL + b, b % 2
                    act.wait_ge(ten[0].sem, ten[0].at(k, TURN))
                    act.wait_ge(ten[0].sem, ten[0].at(k - 1, EXPAND))
                    act_fn(hotT, ps[:, 5, :].bitcast(bf16), ACT.Copy).then_inc(scl[0].sem, 1)
                    act.wait_ge(vec[0].sem, vec[0].at(k, PRED))
                    act.wait_ge(ten[0].sem, ten[0].at(k - 2, SUMS))
                    act_fn(msg[h][:, :, :], mpre[h][:, :, :], ACT.Silu, scale=float(1 / np.sqrt(16 * 8))
                           ).then_inc(scl[0].sem, 1)
                    act.wait_ge(ten[0].sem, ten[0].at(k, SUMS))
                    act.wait_ge(retired, k + 1)
                    act_fn(sc[h][:, :, :], ps[:, 4, 0:P].rearrange("p (u f) -> p u f", f=16),
                           ACT.Copy).then_inc(scl[0].sem, 1)

            n = node["N0"]
            with act.Fori(0, NC) as c:
                one(n, c, 3, st1[0:16, :], ps[0:16, 0, :], ACT.Copy)
                one(n, c, 5, st1[0:16, :], ps[0:16, 1, :], ACT.Copy, scale=0.25)
                one(n, c, 8, wk[:, HE:2 * HE].rearrange("p (r n) -> p r n", r=2), ps[:, 2:4, :], ACT.Copy)
                one(n, c, 11, st1[0:16, :], ps[0:16, 0, :], ACT.Silu, scale=1 / 16.0)
                layernorm(n, c, 15)
                one(n, c, 25, dinv[:, cs(c)], dinv[:, cs(c)], ACT.Sqrt, bias=w["ones"][:, 0:1])
                store_rows(n, c, 30, 16, 1)

            n = node["N1"]
            with act.Fori(0, NC) as c:
                one(n, c, 3, st1[0:64, :], ps[0:64, 0, :], ACT.Identity, bias=w["enc_b0"][:, :])
                store_rows(n, c, 8, 64, 2)
            open_pass(act, scl[2], 2)
            with act.Fori(0, NB) as k:
                act.wait_ge(ten[2].sem, ten[2].at(k, 1))
                act_fn(rst[:, :].rearrange("p (q n) -> p q n", q=2), ps[0:32, 4:6, :], ACT.Relu,
                       bias=w["fb1"][:, :]).then_inc(scl[2].sem, 1)
                act.wait_ge(scl[2].sem, scl[2].at(k, 1))
                act.dma_start(rT[:, ds(k * HE, HE)], rst[:, :]).then_inc(r_out, 16)
                act.wait_ge(r_out, k * 16 + 16)
            n = node["N2"]
            with act.Fori(0, NC) as c:
                one(n, c, 3, st1[:, :], ps[:, 0, :], ACT.Identity, bias=w["enc_b1"][:, :])
                store_rows(n, c, 9, 64, 3)
            n = node["N3"]
            with act.Fori(0, NC) as c:
                one(n, c, 2, st1[0:64, :], gst[0:64, :], ACT.Identity, bias=w["enc_b2"][:, :])
                one(n, c, 5, st1[0:32, :], ps[0:32, 0, :], ACT.Identity, bias=w["lat_b0"][:, :])
                one(n, c, 8, st1[0:3, :], ps[0:3, 1, :], ACT.Identity, bias=w["lat_b1"][:, :])
                one(n, c, 10, st1[0:32, :], ps[0:32, 0, :], ACT.Identity, bias=w["dfc_b0"][:, :])
                one(n, c, 13, st1[0:64, :], ps[0:64, 1, :], ACT.Identity, bias=w["dfc_b1"][:, :])
                store_rows(n, c, 18, 64, 4)
            n = node["N4"]
            with act.Fori(0, NC) as c:
                one(n, c, 3, st1[:, :], ps[:, 0, :], ACT.Identity, bias=w["dec_b0"][:, :])
                store_rows(n, c, 9, 64, 5)
            n = node["N5"]
            with act.Fori(0, NC) as c:
                one(n, c, 2, st1[0:64, :], gst[0:64, :], ACT.Identity, bias=w["dec_b1"][:, :])
                store_rows(n, c, 8, 16, 6)
            n = node["N6"]
            with act.Fori(0, NC) as c:
                one(n, c, 2, st1[0:16, :], gst[0:16, :], ACT.Identity, bias=w["dec_b2"][:, :])
                one(n, c, 4, st1[0:16, :], st2[0:16, :], ACT.Tanh)
                layernorm(n, c, 6)
                store_rows(n, c, 16, 16, 7)

            open_pass(act, scl[7], 7)
            with act.Fori(0, IT) as it:
                for b in range(SL):
                    k, h = it * SL + b, b % 2
                    act.wait_ge(ten[7].sem, ten[7].at(k, 3))
                    act.wait_ge(ten[7].sem, ten[7].at(k - 1, 1))
                    act_fn(sc[h][:, :, :], ps[:, 6, 0:P].rearrange("p (u f) -> p u f", f=16),
                           ACT.Copy).then_inc(scl[7].sem, 1)
            n = node["N7"]
            with act.Fori(0, NC) as c:
                one(n, c, 4, st2[0:16, :], st2[0:16, :], ACT.Identity, bias=w["l2_b"][:, :])
                layernorm(n, c, 5)
                store_rows(n, c, 16, 16, 8)

            for p in (8, 9):
                n = node[PHASES[p + 1]]
                with act.Fori(0, NC) as c:
                    act.wait_ge(n.sem, n.at(c, 3))
                    for g in range(2):
                        act_fn(rzn[:, g, :], ps[0:16, 3 + g, :], ACT.Sigmoid, bias=brz[:, g:g + 1])
                    act_fn(rzn[:, 2, :], ps[0:16, 5, :], ACT.Identity, bias=w["b_hh"][:, 2:3]).then_inc(n.sem, 1)
                    one(n, c, 7, st1[0:16, :], st1[0:16, :], ACT.Tanh, bias=w["b_ih"][:, 2:3])
                    if p == 8:
                        store_rows(n, c, 14, 16, 9)
                    else:
                        layernorm(n, c, 12)
                        store_rows(n, c, 21, 16, 10)

        @block.vector
        def _(dve):
            def one_hot(p, k, h, r):
                if p >= 7:
                    dve.wait_ge(ten[p].sem, ten[p].at(k - 1, 1) if p == 7 else ten[p].at(k - 2, TPER[p]))
                else:
                    dve.wait_ge(ten[p].sem, ten[p].at(k - 1, TPER[p]))
                    k = k + 1
                tt(hot[h][:, :, :], w["iota"][:, :].unsqueeze(1).to_broadcast([P, HT, P]),
                   r[:, ds(k * HT, HT)].unsqueeze(2).to_broadcast([P, HT, P]), ALU.is_equal
                   ).then_inc(vec[p].sem, 1)

            first_node = [dve.alloc_register(f"first_node{u}") for u in range(HT)]

            def load_firsts(k):
                dve.load(first_node, base[0:1, ds(k * HT + HT, HT)])
                return [dve.snap(r, min_val=0, max_val=N) for r in first_node]

            def add_windows(p, k, at, dst, F, first, tiles, window):
                for i, u in enumerate(tiles):
                    v = at[u]
                    dve.wait_ge(vec[p].sem, vec[p].at(k, first + i - 1))
                    tt(dst[0:F, ds(v, P)], dst[0:F, ds(v, P)],
                       window(u), ALU.add).then_inc(vec[p].sem, 1)

            def half_window(h, F):
                return lambda u: ps[0:F, 2 * h + u // 4, (u % 4) * P:(u % 4 + 1) * P]

            def all_added(p):
                dve.wait_ge(vec[p].sem, vec[p].at(NB - 1, VPER[p]))

            def wait(n, c, step):
                dve.wait_ge(n.sem, n.at(c, step - 1))

            def clear(n, c, F):
                ts(acc[0:F, cs(c)], zero[0:F, :], 1.0, None, ALU.mult).then_inc(n.sem, 1)

            def layernorm(n, c, s):
                wait(n, c, s + 1)
                tt(st2[0:16, :], st2[0:16, :], ps[0:16, 0, :], ALU.subtract).then_inc(n.sem, 1)
                wait(n, c, s + 2)
                tt(st1[0:16, :], st2[0:16, :], st2[0:16, :], ALU.mult).then_inc(n.sem, 1)
                wait(n, c, s + 5)
                nc.vector.reciprocal(st1[0:16, :], st1[0:16, :]).then_inc(n.sem, 1)
                wait(n, c, s + 6)
                tt(xT[:, cs(c)], st2[0:16, :], st1[0:16, :], ALU.mult).then_inc(n.sem, 1)

            def leaky(n, c, step, F):
                wait(n, c, step)
                stt(st2[0:F, :], st1[0:F, :], SLOPE, st1[0:F, :], ALU.mult, ALU.max).then_inc(n.sem, 1)

            def scaled(n, c, step, src, F):
                wait(n, c, step)
                tt(gst[0:F, :], src, dinv[0:F, cs(c)], ALU.mult).then_inc(n.sem, 1)

            def keep(n, c, step, F):
                wait(n, c, step)
                ts(acc[0:F, cs(c)], gst[0:F, :], 1.0, None, ALU.mult).then_inc(n.sem, 1)

            nc.vector.memset(acc[:, :], 0.0).then_inc(ready, 1)
            nc.vector.memset(dinv[:, :], 0.0).then_inc(ready, 1)
            nc.vector.memset(invdeg[:, :], 0.0).then_inc(ready, 1)
            nc.vector.memset(ones16[:, :], 1.0).then_inc(ready, 1)
            nc.vector.memset(rel[:, T:], 0.0).then_inc(ready, 1)
            nc.vector.memset(eps[:, :], EPS).then_inc(ready, 1)
            nc.vector.memset(carry[:, :], 0.0).then_inc(ready, 1)
            nc.vector.memset(zero[:, :], 0.0).then_inc(ready, 1)
            dve.wait_ge(w_in, 16 * (len(WEIGHTS) + 4))
            nc.vector.tensor_copy(ident16[:, :], w["ident"][:, :]).then_inc(ready, 1)
            tt(brz[:, :], w["b_ih"][:, 0:2], w["b_hh"][:, 0:2], ALU.add).then_inc(ready, 1)
            tt(rel[:, 0:T], wk[:, 0:T].bitcast(i32), base[:, HT:], ALU.subtract).then_inc(ready, 1)
            tt(rel_last[:, :], wk[:, 0:T].bitcast(i32), rel_last[:, :].bitcast(i32), ALU.is_equal).then_inc(ready, 1)
            dve.wait_ge(ready, 12)
            stt(rel_last[:, :], rel_last[:, :], 4096.0, rel[:, 0:T], ALU.mult, ALU.add).then_inc(ready, 1)
            dve.wait_ge(ready, 13)

            n = node["A0"]
            n.open(dve)
            with dve.Fori(0, NC) as c:
                dve.wait_ge(n.sem, n.at(c, 0))
                ts(gst[0:16, :], xT[:, cs(c)], 1.0, None, ALU.mult).then_inc(n.sem, 1)

            v = vec[0]

            def one_hot16(k, h):
                dve.wait_ge(ten[0].sem, ten[0].at(k - 1, DEGREES))
                tt(hot16[h], w["iota"][:, :].unsqueeze(1).to_broadcast([P, HT, P]),
                   rel[:, ds((k + 1) * HT, HT)].unsqueeze(2).to_broadcast([P, HT, P]), ALU.is_equal
                   ).then_inc(v.sem, 1)

            before = node[PHASES[0]]
            dve.wait_ge(before.sem, before.at(NC - 1, before.per))
            dve.sem_inc(v.sem, (SL - 1) * VPER[0])
            one_hot16(-1, 0)
            dve.wait_ge(v.sem, v.at(-1, HOT))
            dve.sem_inc(v.sem, VPER[0] - 1)
            with dve.Fori(0, IT) as it:
                for b in range(SL):
                    k, h = it * SL + b, b % 2
                    at = load_firsts(k)
                    one_hot16(k, 1 - h)
                    dve.wait_ge(loaded[h], load_count(0, it, b))
                    dve.wait_ge(ten[0].sem, ten[0].at(k - 2, SUMS))
                    tt(same[h][:, :, :], row[h][:, :].bitcast(i32).rearrange("p (u e) -> p u e", e=P),
                       scol[h][:, :].unsqueeze(2).to_broadcast([P, HT, P]), ALU.is_equal).then_inc(v.sem, 1)
                    dve.wait_ge(v.sem, v.at(k, SAME))
                    tt(wk[:, HE:].rearrange("p (u e) -> p u e", e=P), same[h][:, :, :],
                       w["tri"][:, :].unsqueeze(1).to_broadcast([P, HT, P]), ALU.mult).then_inc(v.sem, 1)
                    dve.wait_ge(v.sem, v.at(k, EARLIER))
                    nc.vector.tensor_reduce(tiny[:, 0, :], wk[:, HE:].rearrange("p (u e) -> p u e", e=P), AX,
                                            ALU.add).then_inc(v.sem, 1)
                    dve.wait_ge(v.sem, v.at(k, COUNT))
                    ts(tiny[:, 1, :], tiny[:, 0, :], 1.0, None, ALU.min).then_inc(v.sem, 1)
                    tt(tiny[:, 2, :], w["dummy"][:, 0:1].to_broadcast([P, HT]), scol[h][:, :],
                       ALU.subtract).then_inc(v.sem, 1)
                    dve.wait_ge(v.sem, v.at(k, TODUMMY))
                    tt(tiny[:, 3, :], tiny[:, 1, :], tiny[:, 2, :], ALU.mult).then_inc(v.sem, 1)
                    dve.wait_ge(v.sem, v.at(k, MOVE))
                    dve.wait_ge(retired, k + 1)
                    tt(sidx[h][:, :], tiny[:, 3, :], scol[h][:, :], ALU.add).then_inc(v.sem, 1)
                    dve.wait_ge(ten[0].sem, ten[0].at(k, DEGREES))
                    for u in range(HT):
                        dve.wait_ge(v.sem, v.at(k, SIDX if u < 2 else DEG0 + u - 2))
                        degree = (dinv, invdeg)[u % 2]
                        tt(degree[:, ds(at[u], P)], degree[:, ds(at[u], P)], half_window(h, P)(u), ALU.add
                           ).then_inc(v.sem, 1)
                    dve.wait_ge(ten[0].sem, ten[0].at(k, EXPAND))
                    tt(wk[:, 0:HE].rearrange("p (u h j) -> p u h j", u=HT, h=16),
                       ps[:, 6:8, :].rearrange("p q n -> p (q n)").rearrange("p (u h j) -> p u h j", u=HT, h=16),
                       col[h][:, :].rearrange("p (u j) -> p u j", j=8).unsqueeze(2).to_broadcast([P, HT, 16, 8]),
                       ALU.mult).then_inc(v.sem, 1)
                    dve.wait_ge(v.sem, v.at(k, PMUL))
                    dve.wait_ge(scl[0].sem, scl[0].at(k - 2, SILU))
                    nc.vector.tensor_reduce(mpre[h][:, :, :].rearrange("p u h -> p (u h)"),
                                            wk[:, 0:HE].rearrange("p (x j) -> p x j", j=8), AX, ALU.add
                                            ).then_inc(v.sem, 1)
            all_added(0)

            n = node["N0"]
            n.open(dve)
            with dve.Fori(0, NC) as c:
                dve.wait_ge(tabs_in, c * (16 * NTAB) + 16 * NTAB)
                dve.wait_ge(n.sem, n.at(c, 0))
                nc.vector.tensor_reduce(st2[:, 0:64], wk[:, 0:64 * NTAB].rearrange("p (k f) -> p f k", k=NTAB), AX,
                                        ALU.add).then_inc(n.sem, 1)
                wait(n, c, 6)
                ts(gst[0:16, :], xT[:, cs(c)], 1.0, None, ALU.mult).then_inc(n.sem, 1)
                wait(n, c, 9)
                tt(wk[:, HE:], wk[:, HE:], ps[:, 4:6, :].rearrange("p r n -> p (r n)"), ALU.mult).then_inc(n.sem, 1)
                wait(n, c, 13)
                stt(st2[0:16, :], ps[0:16, 1, :], 0.25, gst[0:16, :], ALU.mult, ALU.add).then_inc(n.sem, 1)
                wait(n, c, 14)
                tt(st2[0:16, :], st2[0:16, :], gst[0:16, :], ALU.add).then_inc(n.sem, 1)
                layernorm(n, c, 15)
                wait(n, c, 22)
                tt(dinv[:, cs(c)], dinv[:, cs(c)], invdeg[:, cs(c)], ALU.add).then_inc(n.sem, 1)
                wait(n, c, 23)
                ts(invdeg[0:16, cs(c)], dinv[0:16, cs(c)], 1.0, None, ALU.max).then_inc(n.sem, 1)
                wait(n, c, 24)
                dve.sem_inc(dve_go, 1)
                nc.vector.reciprocal(invdeg[0:16, cs(c)], invdeg[0:16, cs(c)]).then_inc(n.sem, 1)
                wait(n, c, 26)
                dve.sem_inc(dve_go, 1)
                nc.vector.reciprocal(dinv[:, cs(c)], dinv[:, cs(c)]).then_inc(n.sem, 1)
                scaled(n, c, 27, xT[:, cs(c)], 16)
                keep(n, c, 28, 16)

            def sum_pass(p, F):
                before = node[PHASES[p]]
                dve.wait_ge(before.sem, before.at(NC - 1, before.per))
                dve.sem_inc(vec[p].sem, (SL - 1) * VPER[p])
                one_hot(p, -1, 0, rel)
                dve.wait_ge(vec[p].sem, vec[p].at(-1, HOT))
                dve.sem_inc(vec[p].sem, VPER[p] - 1)
                with dve.Fori(0, IT) as it:
                    for b in range(SL):
                        k, h = it * SL + b, b % 2
                        at = load_firsts(k)
                        one_hot(p, k, 1 - h, rel)
                        dve.wait_ge(ten[p].sem, ten[p].at(k, TPER[p]))
                        add_windows(p, k, at, acc, F, ADD0, range(HT), half_window(h, F))
                all_added(p)

            sum_pass(1, 16)
            n = node["N1"]
            n.open(dve)
            with dve.Fori(0, NC) as c:
                scaled(n, c, 1, acc[0:16, cs(c)], 16)
                leaky(n, c, 4, 64)
                scaled(n, c, 5, st2[0:64, :], 64)
                keep(n, c, 6, 64)
            sum_pass(2, 64)

            def two_layers(name):
                n = node[name]
                n.open(dve)
                with dve.Fori(0, NC) as c:
                    scaled(n, c, 1, acc[0:64, cs(c)], 64)
                    leaky(n, c, 4, 128)
                    scaled(n, c, 6, ps[0:64, 1, :], 64)
                    keep(n, c, 7, 64)

            two_layers("N2")
            sum_pass(3, 64)
            n = node["N3"]
            n.open(dve)
            with dve.Fori(0, NC) as c:
                scaled(n, c, 1, acc[0:64, cs(c)], 64)
                leaky(n, c, 3, 64)
                leaky(n, c, 6, 32)
                leaky(n, c, 11, 32)
                leaky(n, c, 14, 64)
                scaled(n, c, 15, st2[0:64, :], 64)
                keep(n, c, 16, 64)
            sum_pass(4, 64)
            two_layers("N4")
            sum_pass(5, 64)
            n = node["N5"]
            n.open(dve)
            with dve.Fori(0, NC) as c:
                scaled(n, c, 1, acc[0:64, cs(c)], 64)
                leaky(n, c, 3, 64)
                scaled(n, c, 5, ps[0:16, 0, :], 16)
                keep(n, c, 6, 16)
            sum_pass(6, 16)
            n = node["N6"]
            n.open(dve)
            with dve.Fori(0, NC) as c:
                scaled(n, c, 1, acc[0:16, cs(c)], 16)
                leaky(n, c, 3, 16)
                wait(n, c, 5)
                tt(st2[0:16, :], st1[0:16, :], xT[:, cs(c)], ALU.add).then_inc(n.sem, 1)
                layernorm(n, c, 6)
                wait(n, c, 13)
                ts(gst[0:16, :], xT[:, cs(c)], 1.0, None, ALU.mult).then_inc(n.sem, 1)
                clear(n, c, 16)

            ts(sc[1][:, :, :], zero[:, 0:P].rearrange("p (u f) -> p u f", f=16), 1.0, None, ALU.mult).then_inc(ready, 1)
            dve.wait_ge(ready, 14)
            v = vec[7]
            open_pass(dve, v, 7)
            with dve.Fori(0, IT) as it:
                for b in range(SL):
                    k, h = it * SL + b, b % 2
                    at = load_firsts(k - 1)
                    one_hot(7, k, h, rel_last)
                    dve.wait_ge(gathered[7][b], gather_count(it))
                    dve.wait_ge(loaded[h], load_count(7, it, b))
                    dve.wait_ge(ten[7].sem, ten[7].at(k - 2, 2))
                    tt(msg[h][:, :, :], G[b][:, :, 0:16], col[h][:, 0:HT].unsqueeze(2).to_broadcast([P, HT, 16]),
                       ALU.mult).then_inc(v.sem, 1)
                    tt(wk[0:16, 0:HE], row[h][0:16, :].bitcast(i32), prev[h][0:16, :], ALU.not_equal).then_inc(v.sem, 1)
                    dve.wait_ge(v.sem, v.at(k, CHANGED))
                    ts(wk[0:16, 0:HE], wk[0:16, 0:HE], -BIG, None, ALU.mult).then_inc(v.sem, 1)
                    dve.wait_ge(ten[7].sem, ten[7].at(k, 1))
                    add_windows(7, k, at, acc, 16, END0, range(HT), half_window(1 - h, 16))
                    dve.wait_ge(ten[7].sem, ten[7].at(k, 2))
                    dve.wait_ge(ten[7].sem, ten[7].at(k - 1, 3))
                    nc.vector.tensor_tensor_scan(wk[0:16, HE:], wk[0:16, 0:HE],
                                                 ps[0:16, 4:6, :].rearrange("p q n -> p (q n)"),
                                                 carry[:, 0:1], ALU.add, ALU.max).then_inc(v.sem, 1)
                    dve.wait_ge(v.sem, v.at(k, SCAN))
                    nc.vector.tensor_copy(carry[:, :], wk[0:16, 2 * HE - 1:2 * HE]).then_inc(v.sem, 1)
            at = load_firsts(NB - 1)
            dve.wait_ge(ten[7].sem, ten[7].at(NB, 1))
            add_windows(7, NB, at, acc, 16, 1, range(HT), half_window(1, 16))
            dve.wait_ge(vec[7].sem, vec[7].at(NB, HT))
            n = node["N7"]
            n.open(dve)
            with dve.Fori(0, NC) as c:
                dve.wait_ge(n.sem, n.at(c, 0))
                ts(gst[0:16, :], acc[0:16, cs(c)], 1.0, None, ALU.mult).then_inc(n.sem, 1)
                wait(n, c, 3)
                tt(st2[0:16, :], ps[0:16, 3, :], xT[:, cs(c)], ALU.add).then_inc(n.sem, 1)
                layernorm(n, c, 5)
                wait(n, c, 12)
                ts(hT[:, cs(c)], xT[:, cs(c)], 1.0, None, ALU.mult).then_inc(n.sem, 1)
                clear(n, c, 16)
                ts(gst[0:16, :], xT[:, cs(c)], 1.0, None, ALU.mult).then_inc(n.sem, 1)

            for h in range(2):
                nc.vector.memset(row[h][32:33, :], 1.0).then_inc(ready, 1)
            for p in (8, 9):
                v = vec[p]
                ts(msg[1][:, :, :], zero[:, 0:P].rearrange("p (u f) -> p u f", f=16), 1.0, None, ALU.mult
                   ).then_inc(ready, 1)
                dve.wait_ge(ready, 17 + p - 8)
                open_pass(dve, v, p)
                with dve.Fori(0, IT) as it:
                    for b in range(SL):
                        k, h = it * SL + b, b % 2
                        at = load_firsts(k - 1)
                        one_hot(p, k, h, rel)
                        dve.wait_ge(gathered[p][b], gather_count(it))
                        for q in range(4):
                            dve.wait_ge(ten[p].sem, ten[p].at(k, WT[q]))
                            tt(wk[:, q * 512:(q + 1) * 512].rearrange("p (u o i) -> p u o i", u=2, i=16),
                               ps[:, 4 + q, :].rearrange("p (u o i) -> p u o i", u=2, i=16),
                               G[b][:, 2 * q:2 * q + 2, 0:16].unsqueeze(2).to_broadcast([P, 2, 16, 16]),
                               ALU.mult).then_inc(v.sem, 1)
                        dve.wait_ge(v.sem, v.at(k, MUL[3]))
                        nc.vector.tensor_reduce(msg[h][:, :, :].rearrange("p u o -> p (u o)"),
                                                wk[:, :].rearrange("p (x i) -> p x i", i=16), AX, ALU.add
                                                ).then_inc(v.sem, 1)
                        dve.wait_ge(ten[p].sem, ten[p].at(k, WINDOWS8))
                        add_windows(p, k, at, acc, 16, END8, range(HT), half_window(1 - h, 16))
                at = load_firsts(NB - 1)
                dve.wait_ge(ten[p].sem, ten[p].at(NB, 1))
                add_windows(p, NB, at, acc, 16, 1, range(HT), half_window(1, 16))
                dve.wait_ge(v.sem, v.at(NB, HT))
                n = node[PHASES[p + 1]]
                n.open(dve)
                with dve.Fori(0, NC) as c:
                    dve.wait_ge(n.sem, n.at(c, 0))
                    tt(gst[0:16, :], acc[0:16, cs(c)], invdeg[0:16, cs(c)], ALU.mult).then_inc(n.sem, 1)
                    nc.vector.tensor_copy(st2[0:16, :], hT[:, cs(c)]).then_inc(n.sem, 1)
                    wait(n, c, 5)
                    tt(st1[0:16, :], rzn[:, 0, :], rzn[:, 2, :], ALU.mult).then_inc(n.sem, 1)
                    wait(n, c, 6)
                    tt(st1[0:16, :], st1[0:16, :], ps[0:16, 6, :], ALU.add).then_inc(n.sem, 1)
                    wait(n, c, 8)
                    tt(st2[0:16, :], hT[:, cs(c)], st1[0:16, :], ALU.subtract).then_inc(n.sem, 1)
                    wait(n, c, 9)
                    tt(st2[0:16, :], st2[0:16, :], rzn[:, 1, :], ALU.mult).then_inc(n.sem, 1)
                    wait(n, c, 10)
                    tt(hT[:, cs(c)], st2[0:16, :], st1[0:16, :], ALU.add).then_inc(n.sem, 1)
                    wait(n, c, 11)
                    if p == 8:
                        ts(gst[0:16, :], hT[:, cs(c)], 1.0, None, ALU.mult).then_inc(n.sem, 1)
                        clear(n, c, 16)
                    else:
                        tt(st2[0:16, :], hT[:, cs(c)], xT[:, cs(c)], ALU.add).then_inc(n.sem, 1)
                        layernorm(n, c, 12)
                        wait(n, c, 19)
                        ts(gst[0:16, :], xT[:, cs(c)], 1.0, None, ALU.mult).then_inc(n.sem, 1)


def _constants():
    f = np.float32
    i, h = np.arange(256) // 16, np.arange(256) % 16
    return {
        "ident": np.eye(P, dtype=f), "iota": np.tile(np.arange(P, dtype=f), (P, 1)),
        "tri": np.tril(np.ones((P, P), f), -1), "ones": np.ones((P, P), f),
        "mean16": np.full((16, 16), 1 / 16, f), "dummy": (N + np.arange(P, dtype=f))[:, None],
        "rep_i": (np.arange(16)[:, None] == i).astype(f), "rep_h": (np.arange(16)[:, None] == h).astype(f),
    }


def _padded(v, before, after, fill):
    return np.concatenate([np.full(before, fill, v.dtype), v, np.full(after, fill, v.dtype)])


def _layout(x):
    pad = T * P - E
    on_p = lambda v: np.ascontiguousarray(v.reshape(T, P).T)
    rows = lambda v: np.concatenate([v, np.zeros((pad, v.shape[1]), v.dtype)])
    g = {k: np.asarray(v) for k, v in x.items()}
    src, dst = g["src"].astype(np.int32), g["dst"].astype(np.int32)
    far = _padded(dst, 0, pad, FAR)
    a = {
        "xT": np.concatenate([g["x"].T, np.zeros((16, NP - N), np.float32)], 1),
        "src_p": on_p(_padded(src, 0, pad, 0)), "src_r": _padded(src, 0, pad, 0)[None],
        "dst_p": on_p(far), "dst_r": far[None],
        "dst_n": on_p(_padded(dst[1:], 0, pad + 1, FAR)), "prev_r": _padded(dst[:-1], 1, pad, -1)[None],
        "base": _padded(dst[::P], HT, T - len(dst[::P]), 0)[None],
        "ea8": rows(g["edge_attr_8"]).reshape(T, P, 8).transpose(1, 0, 2).reshape(P, T * 8),
        "ea13": rows(g["edge_attr_13"]).T,
        "ew": on_p(_padded(g["edge_weight1"][:, 0], 0, pad, 0)),
        "msg_tp": g["L0_gnn_W_msg_tp"].transpose(0, 2, 1).reshape(16, P), "msg_lin": g["L0_gnn_W_msg_lin"],
        "upd_tp": g["L0_gnn_W_upd_tp"].reshape(2, P, 16).transpose(1, 0, 2).reshape(P, 32),
        "upd_lin": g["L0_gnn_W_upd_lin"],
        "l2_W": g["L2_gnn_W"].T, "l2_b": g["L2_gnn_b"][:, None],
        "f1": g["L3_gnn_fnet_w1"], "fb1": g["L3_gnn_fnet_b1"][:, None],
        "w2b": np.concatenate([g["L3_gnn_fnet_w2"], g["L3_gnn_fnet_b2"][None]]
                              ).reshape(33, 16, 16).transpose(0, 2, 1).reshape(33, 256),
        "w_ih": g["L3_gnn_gru_w_ih"].T, "w_hh": g["L3_gnn_gru_w_hh"].T,
        "b_ih": g["L3_gnn_gru_b_ih"].reshape(3, 16).T, "b_hh": g["L3_gnn_gru_b_hh"].reshape(3, 16).T,
    }
    for part in ("enc", "lat", "dfc", "dec"):
        for i in range(3 if part in ("enc", "dec") else 2):
            a[f"{part}_W{i}"] = g[f"L1_gnn_{part}_W{i}"]
            a[f"{part}_b{i}"] = g[f"L1_gnn_{part}_b{i}"][:, None]
    a.update(_constants())
    return {k: np.ascontiguousarray(v) for k, v in a.items()}


def kernel(**inputs):
    import concourse.bacc as _bacc
    from concourse.bass_utils import run_bass_kernel_spmd as _run

    nc = _bacc.Bacc("TRN2", target_bir_lowering=False, num_devices=1)
    arrays = _layout(inputs)
    aps = {k: nc.dram_tensor("in_" + k, v.shape, mybir.dt.from_np(v.dtype), kind="ExternalInput").ap()
           for k, v in arrays.items()}
    out = nc.dram_tensor("out_0", (NP, 16), mybir.dt.float32, kind="ExternalOutput").ap()
    build(nc, aps, out)
    r = _run(nc, [{"in_" + k: v for k, v in arrays.items()}], core_ids=[0])
    return r.results[0]["out_0"][:N]
```
